# Optimizing a Trainium2 kernel written in Bass

```python
import numpy as np
import jax
import jax.numpy as jnp

def _softmax(x, axis=-1):
    return jax.nn.softmax(x, axis=axis)

def _gelu(x):
    return jax.nn.gelu(x, approximate=True)

def _silu(x):
    return jax.nn.silu(x)

def _sigmoid(x):
    return jax.nn.sigmoid(x)

def _layernorm(x, axis=-1, eps=1e-05):
    m = jnp.mean(x, axis=axis, keepdims=True)
    v = jnp.var(x, axis=axis, keepdims=True)
    return (x - m) / jnp.sqrt(v + eps)

def _scatter_add(tgt, idx, src, axis=0):
    return tgt.at[idx].add(src)

def _segment_sum(src, seg, n):
    return jax.ops.segment_sum(src, seg, n)
kernel_name = 'mk_xattn_ffn_d1_seqx_r8_1d4a5e'

def setup_inputs(seed: int=0):
    np.random.seed(seed)
    _w = jnp.asarray

    def _rec_inputs():
        import jax
        import jax.numpy as jnp
        _rk = jax.random.key(seed)
        x = -0.000125 + 0.9999 * jax.random.normal(jax.random.fold_in(_rk, 1), (4, 256, 128), jnp.float32)
        _lenS = 256 - jax.random.randint(jax.random.fold_in(_rk, 7), (4,), 0, max(1, 256 // 4) + 1, jnp.int32)
        _lenS2 = 512 - jax.random.randint(jax.random.fold_in(_rk, 8), (4,), 0, max(1, 512 // 4) + 1, jnp.int32)
        _ctx_768P = jax.random.normal(jax.random.fold_in(_rk, 11), (4, 16, 96), jnp.float32)
        _ctx_768c = jax.random.dirichlet(jax.random.fold_in(_rk, 511), 0.3 * jnp.ones((16,), jnp.float32), (4, 512))
        _ctx_768t = jnp.einsum('bsk,bkd->bsd', _ctx_768c, _ctx_768P)
        _ctx_768t = _ctx_768t * jax.lax.rsqrt(jnp.mean(jnp.square(_ctx_768t)) + 1e-12) * 0.953939
        ctx_768 = 0.00272024 + 0.999456 * (_ctx_768t + 0.3 * jax.random.normal(jax.random.fold_in(_rk, 611), (4, 512, 96), jnp.float32))
        return (x, ctx_768)
    x, ctx_768 = _rec_inputs()

    def _L0_xattn_setup():
        import jax, jax.numpy as jnp
        import numpy as np
        HEADS = 16
        DIM_HEAD = 64
        SCALE = DIM_HEAD ** (-0.5)
        QUERY_DIM = 128
        CONTEXT_DIM = 96
        INNER_DIM = HEADS * DIM_HEAD
        key = jax.random.key(seed)
        ks = jax.random.split(key, 7)
        B, Nq, Nk = (8, 512, 77)
        x = jax.random.normal(ks[0], (B, Nq, QUERY_DIM), dtype=jnp.float32)
        context = jax.random.normal(ks[1], (B, Nk, CONTEXT_DIM), dtype=jnp.float32)
        Wq = jax.random.normal(ks[2], (QUERY_DIM, INNER_DIM), dtype=jnp.float32) * QUERY_DIM ** (-0.5)
        Wk = jax.random.normal(ks[3], (CONTEXT_DIM, INNER_DIM), dtype=jnp.float32) * CONTEXT_DIM ** (-0.5)
        Wv = jax.random.normal(ks[4], (CONTEXT_DIM, INNER_DIM), dtype=jnp.float32) * CONTEXT_DIM ** (-0.5)
        Wo = jax.random.normal(ks[5], (INNER_DIM, QUERY_DIM), dtype=jnp.float32) * INNER_DIM ** (-0.5)
        bo = jnp.zeros((QUERY_DIM,), dtype=jnp.float32)
        return {'x': x, 'context': context, 'Wq': Wq, 'Wk': Wk, 'Wv': Wv, 'Wo': Wo, 'bo': bo}
    _L0_xattn_all = _L0_xattn_setup()
    _L0_xattn_in = {k: v for k, v in _L0_xattn_all.items() if k in ('Wq', 'Wk', 'Wv', 'Wo', 'bo')}
    del _L0_xattn_all

    def _L0_ffn_setup():
        import jax, jax.numpy as jnp
        import numpy as np
        B, S, D, F, E = (2, 256, 128, 512, 8)
        LN_EPS = 1e-05

        def _xavier(key, shape, fan_in, fan_out):
            a = np.sqrt(6.0 / (fan_in + fan_out))
            return jax.random.uniform(key, shape, jnp.float32, -a, a)
        key = jax.random.key(seed)
        ks = jax.random.split(key, 8)
        tgt = jax.random.normal(ks[0], (B, S, D), jnp.float32)
        router_w = _xavier(ks[1], (E, D), D, E)
        router_b = jnp.zeros((E,), jnp.float32)
        w1 = _xavier(ks[2], (E, D, F), D, F)
        b1 = jnp.zeros((E, F), jnp.float32)
        w2 = _xavier(ks[3], (E, F, D), F, D)
        b2 = jnp.zeros((E, D), jnp.float32)
        gamma = jnp.ones((D,), jnp.float32)
        beta = jnp.zeros((D,), jnp.float32)
        return {'tgt': tgt, 'router_w': router_w, 'router_b': router_b, 'w1': w1, 'b1': b1, 'w2': w2, 'b2': b2, 'gamma': gamma, 'beta': beta}
    _L0_ffn_all = _L0_ffn_setup()
    _L0_ffn_in = {k: v for k, v in _L0_ffn_all.items() if k in ('router_w', 'router_b', 'w1', 'b1', 'w2', 'b2', 'gamma', 'beta')}
    del _L0_ffn_all
    return {'x': x, 'ctx_768': ctx_768, 'L0_xattn_Wq': _L0_xattn_in['Wq'], 'L0_xattn_Wk': _L0_xattn_in['Wk'], 'L0_xattn_Wv': _L0_xattn_in['Wv'], 'L0_xattn_Wo': _L0_xattn_in['Wo'], 'L0_xattn_bo': _L0_xattn_in['bo'], 'L0_ffn_router_w': _L0_ffn_in['router_w'], 'L0_ffn_router_b': _L0_ffn_in['router_b'], 'L0_ffn_w1': _L0_ffn_in['w1'], 'L0_ffn_b1': _L0_ffn_in['b1'], 'L0_ffn_w2': _L0_ffn_in['w2'], 'L0_ffn_b2': _L0_ffn_in['b2'], 'L0_ffn_gamma': _L0_ffn_in['gamma'], 'L0_ffn_beta': _L0_ffn_in['beta']}

def reference(x, ctx_768, L0_xattn_Wq, L0_xattn_Wk, L0_xattn_Wv, L0_xattn_Wo, L0_xattn_bo, L0_ffn_router_w, L0_ffn_router_b, L0_ffn_w1, L0_ffn_b1, L0_ffn_w2, L0_ffn_b2, L0_ffn_gamma, L0_ffn_beta):
    import jax
    import jax.numpy as jnp

    def _L0_xattn_ref(x, context, Wq, Wk, Wv, Wo, bo):
        import jax, jax.numpy as jnp
        import numpy as np
        HEADS = 16
        DIM_HEAD = 64
        SCALE = DIM_HEAD ** (-0.5)
        QUERY_DIM = 128
        CONTEXT_DIM = 96
        INNER_DIM = HEADS * DIM_HEAD
        B, Nq, _ = x.shape
        Nk = context.shape[1]
        q = x @ Wq
        k = context @ Wk
        v = context @ Wv
        q = q.reshape(B, Nq, HEADS, DIM_HEAD).transpose(0, 2, 1, 3)
        k = k.reshape(B, Nk, HEADS, DIM_HEAD).transpose(0, 2, 1, 3)
        v = v.reshape(B, Nk, HEADS, DIM_HEAD).transpose(0, 2, 1, 3)
        sim = jnp.einsum('bhid,bhjd->bhij', q, k) * SCALE
        attn = jax.nn.softmax(sim, axis=-1)
        out = jnp.einsum('bhij,bhjd->bhid', attn, v)
        out = out.transpose(0, 2, 1, 3).reshape(B, Nq, INNER_DIM)
        return out @ Wo + bo

    def _L0_ffn_ref(tgt, router_w, router_b, w1, b1, w2, b2, gamma, beta):
        import jax, jax.numpy as jnp
        import numpy as np
        B, S, D, F, E = (2, 256, 128, 512, 8)
        LN_EPS = 1e-05

        def _xavier(key, shape, fan_in, fan_out):
            a = np.sqrt(6.0 / (fan_in + fan_out))
            return jax.random.uniform(key, shape, jnp.float32, -a, a)
        logits = jnp.einsum('bsd,ed->bse', tgt, router_w) + router_b
        rw = jax.nn.softmax(logits, axis=-1)
        rw = jnp.zeros_like(rw).at[..., 0].set(1.0)
        h = jax.nn.relu(jnp.einsum('bsd,edf->besf', tgt, w1) + b1[None, :, None, :])
        eo = jnp.einsum('besf,efd->besd', h, w2) + b2[None, :, None, :]
        tgt2 = jnp.einsum('besd,bse->bsd', eo, rw)
        x = tgt + tgt2
        mean = jnp.mean(x, axis=-1, keepdims=True)
        var = jnp.mean(jnp.square(x - mean), axis=-1, keepdims=True)
        return (x - mean) * jax.lax.rsqrt(var + LN_EPS) * gamma + beta
    x = x + _L0_xattn_ref(_layernorm(x, axis=-1), ctx_768, L0_xattn_Wq, L0_xattn_Wk, L0_xattn_Wv, L0_xattn_Wo, L0_xattn_bo)
    x = x + _L0_ffn_ref(_layernorm(x, axis=-1), L0_ffn_router_w, L0_ffn_router_b, L0_ffn_w1, L0_ffn_b1, L0_ffn_w2, L0_ffn_b2, L0_ffn_gamma, L0_ffn_beta)
    return x

_drawn_inputs = setup_inputs


def setup_inputs(seed=0):
    import zlib

    import numpy as np

    out = dict(_drawn_inputs(seed))
    spreads = {'L0_xattn_bo': (0.0, 0.1),
     'L0_ffn_router_b': (0.0, 0.1),
     'L0_ffn_b1': (0.0, 0.1),
     'L0_ffn_b2': (0.0, 0.1),
     'L0_ffn_gamma': (1.0, 0.2),
     'L0_ffn_beta': (0.0, 0.1)}
    factors = {}
    for name, (base, spread) in spreads.items():
        noise = np.random.default_rng([zlib.crc32(name.encode()), seed]).standard_normal(out[name].shape)
        drawn = base * np.exp(spread * noise) if base else spread * noise
        out[name] = jnp.asarray(drawn.astype(out[name].dtype))
    for name, factor in factors.items():
        out[name] = (out[name] * factor).astype(out[name].dtype)
    return out
```

```python
from contextlib import ExitStack

import concourse.bass as bass
from concourse import mybir

ALU = mybir.AluOpType
ACT = mybir.ActivationFunctionType
F32 = mybir.dt.float32
F32R = mybir.dt.float32r
AX_X = mybir.AxisListType.X
EPS = 1e-5


def xattn_ffn_kernel(nc, x, ctxT, WqT, WkT, Wv, Wo, bo, w1, b1T, w2, b2, gamma, beta, out):
    P = 128
    N, D = x.shape
    C, NKB = ctxT.shape
    DH, H, _ = WqT.shape
    INNER = H * DH
    F = w1.shape[1]
    B = 4
    NQ, NK = N // B, NKB // B
    PAIRS = H // 2
    UNITS = B * PAIRS
    QT, KT, TT = NQ // P, NK // P, NQ // P
    NT = N // P
    FC = F // P
    GH = 4
    GT = 4
    HALF = INNER // 2
    SCALE = DH ** -0.5
    assert D == P and NK == 512 and QT == 2 and KT == 4 and FC == 4 and PAIRS == 8 and C <= P

    with ExitStack() as ctx:
        def sb(name, shape, dt=F32):
            return ctx.enter_context(nc.sbuf_tensor(name, shape, dt))

        def bank(name):
            return ctx.enter_context(nc.psum_tensor(name, [P, 512], F32))

        def sem(name):
            return ctx.enter_context(nc.semaphore(name))

        x_sb = sb("x_sb", [P, NT, D])
        wqT_sb = sb("wqT_sb", [DH, H, D])
        wkT_sb = sb("wkT_sb", [DH, H, C])
        ctx_sb = sb("ctx_sb", [C, NKB])
        wv_sb = sb("wv_sb", [C, INNER])
        wo_sb = sb("wo_sb", [P, PAIRS, D])
        w1_sb = sb("w1_sb", [D, F])
        w2_sb = sb("w2_sb", [P, FC, D])
        b1_sb = sb("b1_sb", [P, FC])
        rows = sb("rows", [P, 4, D])
        bo_b, b2_b, gamma_b, beta_b = (rows[:, k, :] for k in range(4))

        ctx_hi, ctx_lo = sb("ctx_hi", [C, NKB], F32R), sb("ctx_lo", [C, NKB], F32R)
        wv_hi, wv_lo = sb("wv_hi", [C, INNER], F32R), sb("wv_lo", [C, INNER], F32R)
        a_hi, a_lo = sb("a_hi", [D, H, C], F32R), sb("a_lo", [D, H, C], F32R)
        xnT_hi, xnT_lo = sb("xnT_hi", [D, N], F32R), sb("xnT_lo", [D, N], F32R)
        t_hi, t_lo = sb("t_hi", [C, 2, 2 * NQ], F32R), sb("t_lo", [C, 2, 2 * NQ], F32R)
        cv_hi = [sb(f"cv_hi{h}", [C, NK], F32R) for h in range(2)]
        cv_lo = [sb(f"cv_lo{h}", [C, NK], F32R) for h in range(2)]

        ident = sb("ident", [P, P])
        xn = sb("xn", [P, NT, D])
        values = sb("values", [P, KT, INNER])
        probs = sb("probs", [P, 4, NK])
        probsT = sb("probsT", [P, 2, 2, KT, NQ])
        negmax = sb("negmax", [P, 2, 4])
        den = sb("den", [P, 2, 4])
        rden = sb("rden", [P, 2, 4])
        attnT = sb("attnT", [P, 2, NQ])

        neghalf, eps = sb("neghalf", [P, GT]), sb("eps", [P, GT])
        st1, mv1 = sb("st1", [P, NT, 6]), sb("mv1", [P, NT, 2])
        ve1, rs1 = sb("ve1", [P, NT]), sb("rs1", [P, NT])
        st2, mv2 = sb("st2", [P, TT, 6]), sb("mv2", [P, TT, 2])
        ve2, rs2 = sb("ve2", [P, TT]), sb("rs2", [P, TT])
        st3, mv3 = sb("st3", [P, TT, 6]), sb("mv3", [P, TT, 2])
        ve3, rs3 = sb("ve3", [P, TT]), sb("rs3", [P, TT])
        carrier2, carrier3 = sb("carrier2", [P, 1]), sb("carrier3", [P, 1])
        xbo = sb("xbo", [P, NT, D])
        x2 = sb("x2", [P, TT, D])
        x2b = sb("x2b", [P, TT, D])
        t_sb = sb("t_sb", [P, TT, D])
        tb2 = sb("tb2", [P, TT, D])
        tT = sb("tT", [D, NQ])
        hid = sb("hid", [P, FC, NQ])
        y_sb = sb("y_sb", [P, TT, D])
        z_sb = sb("z_sb", [P, TT, D])
        zg = sb("zg", [P, TT, D])
        out_sb = sb("out_sb", [P, TT, D])

        score_bank = [bank(f"score_bank{i}") for i in range(4)]
        ptr_bank = bank("ptr_bank")
        pv_bank = bank("pv_bank")
        proj_bank = bank("proj_bank")
        wo_bank = bank("wo_bank")

        ld_x, ld_wqk, ld_ctx, ld_wv = sem("ld_x"), sem("ld_wqk"), sem("ld_ctx"), sem("ld_wv")
        ld_wo, ld_ffn, ld_rows = sem("ld_wo"), sem("ld_ffn"), sem("ld_rows")
        ld_cv = [sem("ld_cv0"), sem("ld_cv1")]
        consts_made = sem("consts_made")
        ctx_hi_made, ctx_lo_made = sem("ctx_hi_made"), sem("ctx_lo_made")
        ctx_rest = sem("ctx_rest")
        wv_hi_made, wv_lo_made = sem("wv_hi_made"), sem("wv_lo_made")
        a_done, a_hi_made, a_lo_made = sem("a_done"), sem("a_hi_made"), sem("a_lo_made")
        ln1_stats, ln1_aggr, ln1_eps, ln1_rstd = sem("ln1_stats"), sem("ln1_aggr"), sem("ln1_eps"), sem("ln1_rstd")
        xn_made, xT_done, xT_hi_made, xT_lo_made = sem("xn_made"), sem("xT_done"), sem("xT_hi_made"), sem("xT_lo_made")
        xbo_made = sem("xbo_made")
        proj_done, t_hi_made, t_lo_made = sem("proj_done"), sem("t_hi_made"), sem("t_lo_made")
        v_done, v_kept = sem("v_done"), sem("v_kept")
        scored, maxed, exped = sem("scored"), sem("maxed"), sem("exped")
        rden_made, normed, transposed = sem("rden_made"), sem("normed"), sem("transposed")
        kept_act, kept_dve = sem("kept_act"), sem("kept_dve")
        pv_done, attn_kept, wo_done = sem("pv_done"), sem("attn_kept"), sem("wo_done")
        x2_made, ln2_stats, ln2_aggr, ln2_eps, ln2_rstd = (sem(s) for s in ("x2_made", "ln2_stats", "ln2_aggr", "ln2_eps", "ln2_rstd"))
        t_made, tb2_made = sem("t_made"), sem("tb2_made")
        ffn_done = sem("ffn_done")
        ffn_kept = sem("ffn_kept")
        y_made, ln3_stats, ln3_aggr, ln3_eps, ln3_rstd = (sem(s) for s in ("y_made", "ln3_stats", "ln3_aggr", "ln3_eps", "ln3_rstd"))
        z_made, x2b_made, zg_made, out_made, stored = (sem(s) for s in ("z_made", "x2b_made", "zg_made", "out_made", "stored"))

        def cols(b, n):
            return slice(b * n, b * n + n) if isinstance(b, int) else bass.ds(b * n, n)

        def after(b):
            return nc.s_assert_within(b + 1, 1, B - 1,
                                      skip_runtime_bounds_check_because="used only where b < B - 1")

        def before(b):
            return (b * (B - 1)) // B

        def when(eng, holds, cond, emit):
            if holds:
                emit()
            else:
                with eng.If(cond()):
                    emit()

        block = ctx.enter_context(nc.Block())

        @block.sync
        def _(sp):
            sp.dma_start(x_sb[:, :, :], x.rearrange("(t p) d -> p t d", p=P)).then_inc(ld_x, 16)
            sp.dma_start(wv_sb[:, :], Wv).then_inc(ld_wv, 16)
            for k, row in enumerate((bo, b2, gamma, beta)):
                sp.dma_start(rows[:, k, :], row.partition_broadcast(P)).then_inc(ld_rows, 16)
            sp.dma_start(wo_sb[:, :, :], Wo.rearrange("(q p) d -> p q d", p=P)).then_inc(ld_wo, 16)
            sp.dma_start(w1_sb[:, :], w1).then_inc(ld_ffn, 16)
            sp.dma_start(w2_sb[:, :, :], w2.rearrange("(c p) d -> p c d", p=P)).then_inc(ld_ffn, 16)
            sp.dma_start(b1_sb[:, :], b1T).then_inc(ld_ffn, 16)

            def move_context(half, bb):
                for dst, src in ((cv_hi[half], ctx_hi), (cv_lo[half], ctx_lo)):
                    sp.dma_start(dst[:, :].bitcast(F32), src[:, cols(bb, NK)].bitcast(F32)).then_inc(ld_cv[half], 16)

            sp.wait_ge(ctx_hi_made, 1)
            sp.wait_ge(ctx_lo_made, 1)
            move_context(1, 0)
            with sp.Fori(0, B) as b:
                with sp.If(b < B - 1):
                    sp.wait_ge(ctx_rest, b * 2 + 2)
                    sp.wait_ge(v_done, b * 8 + 4)
                    move_context(0, after(b))
                    sp.wait_ge(v_done, b * 8 + 8)
                    move_context(1, after(b))
                with sp.If(b > 0):
                    sp.wait_ge(out_made, b)
                    sp.dma_start(out[cols(before(b), NQ), :].rearrange("(t p) d -> p t d", p=P),
                                 out_sb[:, :, :]).then_inc(stored, 16)
            sp.wait_ge(out_made, B)
            sp.dma_start(out[(B - 1) * NQ:B * NQ, :].rearrange("(t p) d -> p t d", p=P),
                         out_sb[:, :, :]).then_inc(stored, 16)
            sp.wait_ge(stored, 16 * B)

        @block.gpsimd
        def _(pool):
            nc.gpsimd.memset(ident[:, :], 0.0).then_inc(consts_made, 1)
            nc.gpsimd.memset(neghalf[:, :], -0.5).then_inc(consts_made, 1)
            nc.gpsimd.memset(eps[:, :], EPS).then_inc(consts_made, 1)
            pool.wait_ge(consts_made, 3)
            nc.gpsimd.affine_select(out=ident[:, :], in_=ident[:, :], compare_op=ALU.not_equal, fill=1.0,
                                    base=0, pattern=[[-1, P]], channel_multiplier=1).then_inc(consts_made, 1)
            for g in range(NT // GT):
                tiles = slice(g * GT, g * GT + GT)
                pool.wait_ge(ln1_aggr, g * GT + GT)
                nc.gpsimd.tensor_tensor(ve1[:, tiles], mv1[:, tiles, 1], eps[:, :], ALU.add).then_inc(ln1_eps, 1)
                pool.wait_ge(ln1_eps, g + 1)
                nc.gpsimd.tensor_tensor(rs1[:, tiles], ve1[:, tiles], neghalf[:, :], ALU.pow).then_inc(ln1_rstd, 1)
            pool.wait_ge(ld_ctx, 16)
            for b in range(1, B):
                c = cols(b, NK)
                nc.gpsimd.tensor_copy(ctx_hi[:, c], ctx_sb[:, c]).then_inc(ctx_rest, 1)
                pool.wait_ge(ctx_rest, 2 * b - 1)
                nc.gpsimd.tensor_tensor(ctx_lo[:, c], ctx_sb[:, c], ctx_hi[:, c].bitcast(F32),
                                        ALU.subtract).then_inc(ctx_rest, 1)
            pool.wait_ge(ld_rows, 4 * 16)
            pool.wait_ge(ld_x, 16)
            nc.gpsimd.tensor_tensor(xbo[:, :, :], x_sb[:, :, :],
                                    bo_b.unsqueeze(1).to_broadcast([P, NT, D]), ALU.add).then_inc(xbo_made, 1)

            def per_tile(row):
                return row.unsqueeze(1).to_broadcast([P, TT, D])

            with pool.Fori(0, B) as b:
                pool.wait_ge(ln2_aggr, b * TT + TT)
                nc.gpsimd.tensor_tensor(ve2[:, :], mv2[:, :, 1], eps[:, 0:TT], ALU.add).then_inc(ln2_eps, 1)
                pool.wait_ge(ln2_eps, b + 1)
                nc.gpsimd.tensor_tensor(rs2[:, :], ve2[:, :], neghalf[:, 0:TT], ALU.pow).then_inc(ln2_rstd, 1)
                nc.gpsimd.tensor_tensor(x2b[:, :, :], x2[:, :, :], per_tile(beta_b), ALU.add).then_inc(x2b_made, 1)
                pool.wait_ge(t_made, b * TT + TT)
                nc.gpsimd.tensor_tensor(tb2[:, :, :], t_sb[:, :, :], per_tile(b2_b), ALU.add).then_inc(tb2_made, 1)
                pool.wait_ge(ln3_aggr, b * TT + TT)
                nc.gpsimd.tensor_tensor(ve3[:, :], mv3[:, :, 1], eps[:, 0:TT], ALU.add).then_inc(ln3_eps, 1)
                pool.wait_ge(ln3_eps, b + 1)
                nc.gpsimd.tensor_tensor(rs3[:, :], ve3[:, :], neghalf[:, 0:TT], ALU.pow).then_inc(ln3_rstd, 1)
                pool.wait_ge(z_made, b * TT + TT)
                nc.gpsimd.tensor_tensor(zg[:, :, :], z_sb[:, :, :], per_tile(gamma_b), ALU.mult).then_inc(zg_made, 1)
                pool.wait_ge(zg_made, b + 1)
                pool.wait_ge(x2b_made, b + 1)
                pool.wait_ge(stored, b * 16)
                nc.gpsimd.tensor_tensor(out_sb[:, :, :], zg[:, :, :], x2b[:, :, :], ALU.add).then_inc(out_made, 1)

        @block.scalar
        def _(act):
            act.dma_start(wqT_sb[:, :, :], WqT).then_inc(ld_wqk, 16)
            act.dma_start(wkT_sb[:, :, :], WkT).then_inc(ld_wqk, 16)
            act.dma_start(ctx_sb[:, :], ctxT).then_inc(ld_ctx, 16)

            def keep_a_hi(g):
                act.wait_ge(a_done, g + 1)
                nc.scalar.activation(a_hi[:, GH * g:GH * g + GH, :].rearrange("d h c -> d (h c)"),
                                     score_bank[g][:, 0:GH * C], ACT.Copy, scale=SCALE).then_inc(a_hi_made, 1)

            def keep_xT_hi(g, src):
                act.wait_ge(xT_done, g + 1)
                nc.scalar.activation(xnT_hi[:, 512 * g:512 * g + 512], src[:, :], ACT.Copy).then_inc(xT_hi_made, 1)

            def keep_t_hi(u, par):
                act.wait_ge(proj_done, u + 1)
                nc.scalar.activation(t_hi[:, par, :], proj_bank[0:C, :], ACT.Copy).then_inc(t_hi_made, 1)

            def keep_values(n, half, kt):
                act.wait_ge(v_done, n + 1)
                nc.scalar.activation(values[:, kt, half * HALF:half * HALF + HALF], proj_bank[:, :],
                                     ACT.Copy).then_inc(v_kept, 1)

            def exp_tile(n, par, i):
                act.wait_ge(maxed, n + 1)
                nc.scalar.activation(probs[:, i, :], score_bank[i][:, :], ACT.Exp, bias=negmax[:, par, i:i + 1],
                                     accum_out=den[:, par, i:i + 1]).then_inc(exped, 1)

            def keep_transposed(n, par, i):
                h, qt = i // QT, i % QT
                act.wait_ge(transposed, n + 1)
                nc.scalar.activation(probsT[:, par, h, :, qt * P:qt * P + P],
                                     ptr_bank[:, :].rearrange("k (t q) -> k t q", t=KT),
                                     ACT.Copy).then_inc(kept_act, 1)

            def keep_tT(fb):
                act.wait_ge(ffn_done, fb * 4 + 1)
                nc.scalar.activation(tT[:, :], pv_bank[:, 0:NQ], ACT.Copy).then_inc(ffn_kept, 1)

            def keep_hidden(fb, k):
                act.wait_ge(ffn_done, fb * 4 + 2 + k)
                for j in range(2):
                    c = 2 * k + j
                    ins = nc.scalar.activation(hid[:, c, :], pv_bank[:, j * NQ:j * NQ + NQ], ACT.Relu,
                                               bias=b1_sb[:, c:c + 1])
                ins.then_inc(ffn_kept, 1)

            act.wait_ge(ld_ctx, 16)
            nc.scalar.activation(ctx_hi[:, 0:NK], ctx_sb[:, 0:NK], ACT.Copy).then_inc(ctx_hi_made, 1)
            act.wait_ge(ld_wv, 16)
            for half in range(2):
                c = slice(half * HALF, half * HALF + HALF)
                nc.scalar.activation(wv_hi[:, c], wv_sb[:, c], ACT.Copy).then_inc(wv_hi_made, 1)
            keep_a_hi(0)
            keep_xT_hi(0, ptr_bank)
            for g in range(1, H // GH):
                keep_a_hi(g)
            keep_t_hi(0, 0)
            keep_xT_hi(1, pv_bank)
            keep_values(0, 0, 0)
            keep_t_hi(1, 1)
            keep_values(1, 0, 1)
            exp_tile(0, 0, 0)
            exp_tile(1, 0, 1)
            keep_values(2, 0, 2)
            exp_tile(2, 0, 2)
            exp_tile(3, 0, 3)
            keep_values(3, 0, 3)
            act.wait_ge(ld_ffn, 3 * 16)

            with act.Fori(0, B) as b:
                for p in range(PAIRS):
                    par, nxt = p % 2, (p + 1) % 2
                    n = b * (4 * PAIRS) + 4 * p
                    for i in range(4):
                        if i < 3:
                            keep_transposed(n + i, par, i)

                        def next_exp():
                            if i == 3:
                                act.wait_ge(transposed, n + 4)
                            exp_tile(n + 4 + i, nxt, i)
                        when(act, p < PAIRS - 1, lambda: b < B - 1, next_exp)
                        if i == 0:
                            when(act, p < PAIRS - 2, lambda: b < B - 1,
                                 lambda: keep_t_hi(b * PAIRS + p + 2, par))
                        if i == 2:
                            when(act, p < 4, lambda: b < B - 1,
                                 lambda: keep_values(b * 8 + 4 + p, 1 if p < 4 else 0, p % 4))
                    if p == 3:
                        when(act, False, lambda: b > 0, lambda: keep_tT(before(b)))
                    if p in (4, 5):
                        when(act, False, lambda: b > 0, lambda: keep_hidden(before(b), p - 4))
            keep_tT(B - 1)
            keep_hidden(B - 1, 0)
            keep_hidden(B - 1, 1)

        @block.vector
        def _(dve):
            def stats(st, mv, src, tiles, s_stats, s_aggr, base, carrier=None):
                for k, t in enumerate(tiles):
                    nc.vector.bn_stats(st[:, t, :], src[:, t, :]).then_inc(s_stats, 1)
                for k, t in enumerate(tiles):
                    if isinstance(base, int):
                        dve.wait_ge(s_stats, base + k + 1)
                    elif k == 0:
                        dve.wait_ge(s_stats, base + len(tiles))
                        nc.vector.memset(carrier[:, :], 0.0)
                    nc.vector.bn_aggr(mv[:, t, :], st[:, t, :]).then_inc(s_aggr, 1)

            def apply_norm(dst, src, mv, rs, t, s_made):
                nc.vector.tensor_scalar(dst[:, t, :], src[:, t, :], mv[:, t, 0:1], rs[:, t:t + 1],
                                        ALU.subtract, ALU.mult).then_inc(s_made, 1)

            def low_half(lo, full, hi, s_made):
                nc.vector.tensor_tensor(lo, full, hi.bitcast(F32), ALU.subtract).then_inc(s_made, 1)

            def keep_a_lo(g):
                heads = slice(GH * g, GH * g + GH)
                dve.wait_ge(a_hi_made, g + 1)
                nc.vector.scalar_tensor_tensor(out=a_lo[:, heads, :].rearrange("d h c -> d (h c)"),
                                               in0=score_bank[g][:, 0:GH * C], scalar=SCALE,
                                               in1=a_hi[:, heads, :].rearrange("d h c -> d (h c)").bitcast(F32),
                                               op0=ALU.mult, op1=ALU.subtract).then_inc(a_lo_made, 1)

            def keep_xT_lo(g, src):
                c = slice(512 * g, 512 * g + 512)
                dve.wait_ge(xT_hi_made, g + 1)
                low_half(xnT_lo[:, c], src[:, :], xnT_hi[:, c], xT_lo_made)

            def keep_t_lo(u, par):
                dve.wait_ge(t_hi_made, u + 1)
                low_half(t_lo[:, par, :], proj_bank[0:C, :], t_hi[:, par, :], t_lo_made)

            def row_max(n, par, i):
                dve.wait_ge(scored, n + 1)
                nc.vector.tensor_reduce(negmax[:, par, i:i + 1], score_bank[i][:, :], AX_X, ALU.max,
                                        negate=True).then_inc(maxed, 1)

            def row_rden(n, par, i):
                dve.wait_ge(exped, n + 1)
                nc.vector.reciprocal(rden[:, par, i:i + 1], den[:, par, i:i + 1]).then_inc(rden_made, 1)

            def row_norm(n, par, i):
                dve.wait_ge(rden_made, n + 1)
                nc.vector.tensor_scalar(probs[:, i, :], probs[:, i, :], rden[:, par, i:i + 1], None,
                                        ALU.mult).then_inc(normed, 1)

            def keep_transposed(n, par, i):
                h, qt = i // QT, i % QT
                dve.wait_ge(transposed, n + 1)
                nc.vector.tensor_copy(probsT[:, par, h, :, qt * P:qt * P + P],
                                      ptr_bank[:, :].rearrange("k (t q) -> k t q", t=KT)).then_inc(kept_dve, 1)

            def keep_attn(u, par):
                dve.wait_ge(pv_done, u + 1)
                nc.vector.tensor_copy(attnT[:, par, :], pv_bank[:, 0:NQ]).then_inc(attn_kept, 1)

            def residual(fb):
                dve.wait_ge(wo_done, fb * PAIRS + PAIRS)
                dve.wait_ge(xbo_made, 1)
                dve.wait_ge(out_made, fb)
                xr = xbo[:, 2 * fb:2 * fb + TT, :] if isinstance(fb, int) else xbo[:, bass.ds(fb * TT, TT), :]
                nc.vector.tensor_tensor(x2[:, :, :], wo_bank[:, 0:NQ].rearrange("p (t d) -> p t d", t=TT), xr,
                                        ALU.add).then_inc(x2_made, 1)
                dve.wait_ge(x2_made, fb + 1)
                stats(st2, mv2, x2, range(TT), ln2_stats, ln2_aggr, fb * TT, carrier2)

            def norm2(fb):
                dve.wait_ge(ln2_rstd, fb + 1)
                for t in range(TT):
                    apply_norm(t_sb, x2, mv2, rs2, t, t_made)

            def finish_y(fb):
                dve.wait_ge(ffn_done, fb * 4 + 4)
                dve.wait_ge(tb2_made, fb + 1)
                nc.vector.tensor_tensor(y_sb[:, :, :], pv_bank[:, 0:NQ].rearrange("p (t d) -> p t d", t=TT),
                                        tb2[:, :, :], ALU.add).then_inc(ffn_kept, 1)
                dve.wait_ge(ffn_kept, fb * 4 + 8)
                stats(st3, mv3, y_sb, range(TT), ln3_stats, ln3_aggr, fb * TT, carrier3)

            def norm3(fb):
                dve.wait_ge(ln3_rstd, fb + 1)
                for t in range(TT):
                    apply_norm(z_sb, y_sb, mv3, rs3, t, z_made)

            nc.vector.memset(hid[:, :, :], 0.0).then_inc(ffn_kept, 4)

            dve.wait_ge(ld_x, 16)
            stats(st1, mv1, x_sb, range(0, GT), ln1_stats, ln1_aggr, 0)
            stats(st1, mv1, x_sb, range(GT, NT), ln1_stats, ln1_aggr, GT)
            dve.wait_ge(ctx_hi_made, 1)
            low_half(ctx_lo[:, 0:NK], ctx_sb[:, 0:NK], ctx_hi[:, 0:NK], ctx_lo_made)
            dve.wait_ge(ln1_rstd, 1)
            for t in range(GT):
                apply_norm(xn, x_sb, mv1, rs1, t, xn_made)
            for half in range(2):
                c = slice(half * HALF, half * HALF + HALF)
                dve.wait_ge(wv_hi_made, half + 1)
                low_half(wv_lo[:, c], wv_sb[:, c], wv_hi[:, c], wv_lo_made)
            keep_a_lo(0)
            keep_xT_lo(0, ptr_bank)
            for g in range(1, H // GH):
                keep_a_lo(g)
            keep_t_lo(0, 0)
            dve.wait_ge(ln1_rstd, 2)
            for t in range(GT, NT):
                apply_norm(xn, x_sb, mv1, rs1, t, xn_made)
            keep_xT_lo(1, pv_bank)
            keep_t_lo(1, 1)
            for i in range(4):
                row_max(i, 0, i)
                if i:
                    row_rden(i - 1, 0, i - 1)
                    row_norm(i - 1, 0, i - 1)

            with dve.Fori(0, B) as b:
                for p in range(PAIRS):
                    par, nxt = p % 2, (p + 1) % 2
                    n = b * (4 * PAIRS) + 4 * p
                    for i in range(4):
                        def scores_part():
                            if i:
                                row_rden(n + 4 + i - 1, nxt, i - 1)
                            row_max(n + 4 + i, nxt, i)
                            if i:
                                row_norm(n + 4 + i - 1, nxt, i - 1)
                        if i == 0:
                            row_rden(n + 3, par, 3)
                        when(dve, p < PAIRS - 1, lambda: b < B - 1, scores_part)
                        if i == 0:
                            row_norm(n + 3, par, 3)
                            when(dve, p < PAIRS - 2, lambda: b < B - 1,
                                 lambda: keep_t_lo(b * PAIRS + p + 2, par))
                            if p == 7:
                                when(dve, False, lambda: b > 0, lambda: finish_y(before(b)))
                        if i == 1:
                            when(dve, p > 0, lambda: b > 0, lambda: keep_attn(b * PAIRS + p - 1, nxt))
                        if i == 3:
                            keep_transposed(n + 3, par, 3)
                    if p == 0:
                        when(dve, False, lambda: b > 0, lambda: residual(before(b)))
                    if p == 1:
                        when(dve, False, lambda: b > 0, lambda: norm2(before(b)))
                    if p == 7:
                        when(dve, False, lambda: b > 0, lambda: norm3(before(b)))
            keep_attn(UNITS - 1, 1)
            residual(B - 1)
            norm2(B - 1)
            finish_y(B - 1)
            norm3(B - 1)

        @block.tensor
        def _(pe):
            def three(dst, w, m, start=True):
                (w_hi, w_lo), (m_hi, m_lo) = w, m
                nc.tensor.matmul(dst, w_hi, m_hi, start=start, stop=False)
                nc.tensor.matmul(dst, w_hi, m_lo, start=False, stop=False)
                return nc.tensor.matmul(dst, w_lo, m_hi, start=False, stop=True)

            def make_a(g):
                for j in range(GH):
                    h = GH * g + j
                    ins = nc.tensor.matmul(score_bank[g][:, j * C:j * C + C], wqT_sb[:, h, :], wkT_sb[:, h, :],
                                           start=True, stop=True)
                ins.then_inc(a_done, 1)

            def transpose_x(g, dst):
                pe.wait_ge(xn_made, GT * g + GT)
                for j in range(GT):
                    ins = nc.tensor.transpose(dst[:, j * P:j * P + P], xn[:, GT * g + j, :], ident[:, :])
                ins.then_inc(xT_done, 1)

            def project(p, bb):
                for h in range(2):
                    hh = 2 * p + h
                    ins = three(proj_bank[0:C, h * NQ:h * NQ + NQ], (a_hi[:, hh, :], a_lo[:, hh, :]),
                                (xnT_hi[:, cols(bb, NQ)], xnT_lo[:, cols(bb, NQ)]))
                ins.then_inc(proj_done, 1)

            def value_piece(chi, clo, half, kt):
                k, c = slice(kt * P, kt * P + P), slice(half * HALF, half * HALF + HALF)
                three(proj_bank[:, :], (chi[:, k], clo[:, k]), (wv_hi[:, c], wv_lo[:, c])).then_inc(v_done, 1)

            def score(par, i, bb):
                h, qt = i // QT, i % QT
                q = slice(h * NQ + qt * P, h * NQ + qt * P + P)
                three(score_bank[i][:, :], (t_hi[:, par, q], t_lo[:, par, q]),
                      (ctx_hi[:, cols(bb, NK)], ctx_lo[:, cols(bb, NK)])).then_inc(scored, 1)

            def transpose_probs(i):
                for kt in range(KT):
                    ins = nc.tensor.transpose(ptr_bank[:, kt * P:kt * P + P], probs[:, i, kt * P:kt * P + P],
                                              ident[:, :])
                ins.then_inc(transposed, 1)

            def times_values(p, par):
                for kt in range(KT):
                    for h in range(2):
                        c = (2 * p + h) * DH
                        ins = nc.tensor.matmul(pv_bank[h * DH:h * DH + DH, 0:NQ], values[:, kt, c:c + DH],
                                               probsT[:, par, h, kt, :], start=(kt == 0), stop=(kt == KT - 1))
                ins.then_inc(pv_done, 1)

            def out_project(p, par):
                for t in range(TT):
                    ins = nc.tensor.matmul(wo_bank[:, t * D:t * D + D], attnT[:, par, t * P:t * P + P],
                                           wo_sb[:, p, :], start=(p == 0 and t == 0), stop=(p == PAIRS - 1),
                                           skip_group_check=True)
                ins.then_inc(wo_done, 1)

            def ffn_piece(k, fb):
                if k == 0:
                    pe.wait_ge(t_made, fb * TT + TT)
                    for t in range(TT):
                        ins = nc.tensor.transpose(pv_bank[:, t * P:t * P + P], t_sb[:, t, :], ident[:, :])
                elif k < 3:
                    pe.wait_ge(ffn_kept, fb * 4 + 4 + k)
                    for j in range(2):
                        c = 2 * (k - 1) + j
                        ins = nc.tensor.matmul(pv_bank[:, j * NQ:j * NQ + NQ], w1_sb[:, c * P:c * P + P], tT[:, :],
                                               start=True, stop=True)
                else:
                    pe.wait_ge(ffn_kept, fb * 4 + 4 + 3)
                    for t in range(TT):
                        for c in range(FC):
                            ins = nc.tensor.matmul(pv_bank[:, t * D:t * D + D], hid[:, c, t * P:t * P + P],
                                                   w2_sb[:, c, :], start=(c == 0), stop=(c == FC - 1))
                ins.then_inc(ffn_done, 1)

            pe.wait_ge(ld_wqk, 32)
            for g in range(H // GH):
                make_a(g)
            pe.wait_ge(consts_made, 4)
            transpose_x(0, ptr_bank)
            pe.wait_ge(a_lo_made, 1)
            pe.wait_ge(xT_lo_made, 1)
            project(0, 0)
            transpose_x(1, pv_bank)
            pe.wait_ge(ctx_lo_made, 1)
            pe.wait_ge(wv_lo_made, 2)
            pe.wait_ge(t_lo_made, 1)
            value_piece(ctx_hi, ctx_lo, 0, 0)
            pe.wait_ge(v_kept, 1)
            project(1, 0)
            pe.wait_ge(t_lo_made, 2)
            value_piece(ctx_hi, ctx_lo, 0, 1)
            pe.wait_ge(a_lo_made, 4)
            score(0, 0, 0)
            score(0, 1, 0)
            pe.wait_ge(v_kept, 2)
            value_piece(ctx_hi, ctx_lo, 0, 2)
            score(0, 2, 0)
            score(0, 3, 0)
            pe.wait_ge(v_kept, 3)
            value_piece(ctx_hi, ctx_lo, 0, 3)
            pe.wait_ge(xT_lo_made, 2)
            pe.wait_ge(ld_wo, 16)
            pe.wait_ge(ld_ffn, 3 * 16)

            with pe.Fori(0, B) as b:
                for p in range(PAIRS):
                    par, nxt = p % 2, (p + 1) % 2
                    u = b * PAIRS + p
                    n = b * (4 * PAIRS) + 4 * p
                    for i in range(4):
                        def next_score():
                            pe.wait_ge(exped, n + i + 1)
                            if i == 0:
                                pe.wait_ge(t_lo_made, u + 2)
                                if p == PAIRS - 1:
                                    pe.wait_ge(ctx_rest, b * 2 + 2)
                            score(nxt, i, after(b) if p == PAIRS - 1 else b)
                        when(pe, p < PAIRS - 1, lambda: b < B - 1, next_score)

                        pe.wait_ge(normed, n + i + 1)
                        if i == 0:
                            pe.wait_ge(kept_dve, u)
                        else:
                            pe.wait_ge(kept_act, u * 3 + i)
                        transpose_probs(i)

                        if i == 0:
                            def next_project():
                                if p == 5:
                                    with pe.If(b < B - 1):
                                        pe.wait_ge(v_kept, b * 8 + 4 + p)
                                else:
                                    pe.wait_ge(v_kept, b * 8 + 4 + p)
                                project((p + 2) % PAIRS, b if p < PAIRS - 2 else after(b))
                            when(pe, p < PAIRS - 2, lambda: b < B - 1, next_project)
                        if i == 1:
                            def prev_values():
                                pe.wait_ge(kept_act, u * 3)
                                pe.wait_ge(kept_dve, u)
                                if p in (1, 5):
                                    pe.wait_ge(v_kept, b * 8 + 4 + p - 1)
                                if p >= 4:
                                    pe.wait_ge(ffn_kept, b * 4 + p - 3)
                                times_values((p - 1) % PAIRS, nxt)
                            when(pe, p > 0, lambda: b > 0, prev_values)
                        if i == 2:
                            def next_value_piece():
                                pe.wait_ge(t_lo_made, u + 3)
                                half = 1 if p < 4 else 0
                                pe.wait_ge(ld_cv[half], (b + 1) * 32)
                                value_piece(cv_hi[half], cv_lo[half], half, p % 4)
                            when(pe, p < 4, lambda: b < B - 1, next_value_piece)
                        if i == 3:
                            def prev_project():
                                pe.wait_ge(attn_kept, u)
                                if p == 1:
                                    pe.wait_ge(x2_made, b)
                                out_project((p - 1) % PAIRS, nxt)
                            when(pe, p > 0, lambda: b > 0, prev_project)
                            if 3 <= p <= 6:
                                when(pe, False, lambda: b > 0, lambda: ffn_piece(p - 3, before(b)))
            pe.wait_ge(kept_act, UNITS * 3)
            pe.wait_ge(kept_dve, UNITS)
            times_values(PAIRS - 1, 1)
            pe.wait_ge(attn_kept, UNITS)
            out_project(PAIRS - 1, 1)
            for k in range(4):
                if k == 2:
                    pe.wait_ge(ffn_kept, (B - 1) * 4 + 4 + 2)
                ffn_piece(k, B - 1)


def kernel(x, ctx_768, L0_xattn_Wq, L0_xattn_Wk, L0_xattn_Wv, L0_xattn_Wo, L0_xattn_bo,
           L0_ffn_router_w, L0_ffn_router_b, L0_ffn_w1, L0_ffn_b1, L0_ffn_w2, L0_ffn_b2,
           L0_ffn_gamma, L0_ffn_beta):
    import numpy as np
    import concourse.bacc as bacc
    from concourse.bass_utils import run_bass_kernel_spmd

    B, NQ, D = x.shape
    C = ctx_768.shape[2]
    H, DH, P = 16, 64, 128
    Wq, Wk = np.asarray(L0_xattn_Wq), np.asarray(L0_xattn_Wk)
    arrays = {
        "x": np.asarray(x).reshape(B * NQ, D),
        "ctxT": np.asarray(ctx_768).transpose(2, 0, 1).reshape(C, -1),
        "WqT": Wq.reshape(D, H, DH).transpose(2, 1, 0),
        "WkT": Wk.reshape(C, H, DH).transpose(2, 1, 0),
        "Wv": np.asarray(L0_xattn_Wv),
        "Wo": np.asarray(L0_xattn_Wo),
        "bo": np.asarray(L0_xattn_bo),
        "w1": np.asarray(L0_ffn_w1)[0],
        "b1T": np.asarray(L0_ffn_b1)[0].reshape(-1, P).T,
        "w2": np.asarray(L0_ffn_w2)[0],
        "b2": np.asarray(L0_ffn_b2)[0],
        "gamma": np.asarray(L0_ffn_gamma),
        "beta": np.asarray(L0_ffn_beta),
    }
    arrays = {f"in_{k}": np.ascontiguousarray(v) for k, v in arrays.items()}
    nc = bacc.Bacc("TRN2", target_bir_lowering=False, num_devices=1)
    args = [nc.dram_tensor(k, v.shape, mybir.dt.from_np(v.dtype), kind="ExternalInput").ap()
            for k, v in arrays.items()]
    args.append(nc.dram_tensor("out", (B * NQ, D), F32, kind="ExternalOutput").ap())
    xattn_ffn_kernel(nc, *args)
    r = run_bass_kernel_spmd(nc, [arrays], core_ids=[0])
    return r.results[0]["out"].reshape(B, NQ, D)
```

```python
from contextlib import ExitStack

import concourse.bass as bass
from concourse import mybir

ALU = mybir.AluOpType
ACT = mybir.ActivationFunctionType
F32 = mybir.dt.float32
F32R = mybir.dt.float32r
AX_X = mybir.AxisListType.X
EPS = 1e-5


def xattn_ffn_kernel(nc, x, ctxT, WqT, WkT, Wv, Wo, bo, w1, b1T, w2, b2, gamma, beta, out):
    P = 128
    N, D = x.shape
    C, NKB = ctxT.shape
    DH, H, _ = WqT.shape
    INNER = H * DH
    F = w1.shape[1]
    B = 4
    NQ, NK = N // B, NKB // B
    PAIRS = H // 2
    UNITS = B * PAIRS
    QT, KT, TT = NQ // P, NK // P, NQ // P
    NT = N // P
    FC = F // P
    GH = 4
    GT = 4
    HALF = INNER // 2
    SCALE = DH ** -0.5
    assert D == P and NK == 512 and QT == 2 and KT == 4 and FC == 4 and PAIRS == 8 and C <= P

    with ExitStack() as ctx:
        def sb(name, shape, dt=F32):
            return ctx.enter_context(nc.sbuf_tensor(name, shape, dt))

        def bank(name):
            return ctx.enter_context(nc.psum_tensor(name, [P, 512], F32))

        def sem(name):
            return ctx.enter_context(nc.semaphore(name))

        x_sb = sb("x_sb", [P, NT, D])
        wqT_sb = sb("wqT_sb", [DH, H, D])
        wkT_sb = sb("wkT_sb", [DH, H, C])
        ctx_sb = sb("ctx_sb", [C, NKB])
        wv_sb = sb("wv_sb", [C, INNER])
        wo_sb = sb("wo_sb", [P, PAIRS, D])
        w1_sb = sb("w1_sb", [D, F])
        w2_sb = sb("w2_sb", [P, FC, D])
        b1_sb = sb("b1_sb", [P, FC])
        rows = sb("rows", [P, 4, D])
        bo_b, b2_b, gamma_b, beta_b = (rows[:, k, :] for k in range(4))

        ctx_hi, ctx_lo = sb("ctx_hi", [C, NKB], F32R), sb("ctx_lo", [C, NKB], F32R)
        wv_hi, wv_lo = sb("wv_hi", [C, INNER], F32R), sb("wv_lo", [C, INNER], F32R)
        a_hi, a_lo = sb("a_hi", [D, H, C], F32R), sb("a_lo", [D, H, C], F32R)
        xnT_hi, xnT_lo = sb("xnT_hi", [D, N], F32R), sb("xnT_lo", [D, N], F32R)
        t_hi, t_lo = sb("t_hi", [C, 2, 2 * NQ], F32R), sb("t_lo", [C, 2, 2 * NQ], F32R)
        cv_hi = [sb(f"cv_hi{h}", [C, NK], F32R) for h in range(2)]
        cv_lo = [sb(f"cv_lo{h}", [C, NK], F32R) for h in range(2)]

        ident = sb("ident", [P, P])
        xn = sb("xn", [P, NT, D])
        values = sb("values", [P, KT, INNER])
        probs = sb("probs", [P, 4, NK])
        probsT = sb("probsT", [P, 2, 2, KT, NQ])
        negmax = sb("negmax", [P, 2, 4])
        den = sb("den", [P, 2, 4])
        rden = sb("rden", [P, 2, 4])
        attnT = sb("attnT", [P, 2, NQ])

        neghalf, eps = sb("neghalf", [P, GT]), sb("eps", [P, GT])
        st1, mv1 = sb("st1", [P, NT, 6]), sb("mv1", [P, NT, 2])
        ve1, rs1 = sb("ve1", [P, NT]), sb("rs1", [P, NT])
        st2, mv2 = sb("st2", [P, TT, 6]), sb("mv2", [P, TT, 2])
        ve2, rs2 = sb("ve2", [P, TT]), sb("rs2", [P, TT])
        st3, mv3 = sb("st3", [P, TT, 6]), sb("mv3", [P, TT, 2])
        ve3, rs3 = sb("ve3", [P, TT]), sb("rs3", [P, TT])
        carrier2, carrier3 = sb("carrier2", [P, 1]), sb("carrier3", [P, 1])
        credits = sb("credits", [P, 4])
        xbo = sb("xbo", [P, NT, D])
        x2 = sb("x2", [P, TT, D])
        x2b = sb("x2b", [P, TT, D])
        t_sb = sb("t_sb", [P, TT, D])
        tb2 = sb("tb2", [P, TT, D])
        tT = sb("tT", [D, NQ])
        hid = sb("hid", [P, FC, NQ])
        y_sb = sb("y_sb", [P, TT, D])
        yg = sb("yg", [P, TT, D])
        out_sb = sb("out_sb", [P, NT, D])

        score_bank = [bank(f"score_bank{i}") for i in range(4)]
        ptr_bank = bank("ptr_bank")
        pv_bank = bank("pv_bank")
        proj_bank = bank("proj_bank")
        wo_bank = bank("wo_bank")

        ld_x, ld_wqk, ld_ctx, ld_wv = sem("ld_x"), sem("ld_wqk"), sem("ld_ctx"), sem("ld_wv")
        ld_wo, ld_ffn, ld_rows = sem("ld_wo"), sem("ld_ffn"), sem("ld_rows")
        ld_cv = [sem("ld_cv0"), sem("ld_cv1")]
        consts_made = sem("consts_made")
        ctx_hi_made, ctx_lo_made = sem("ctx_hi_made"), sem("ctx_lo_made")
        ctx_rest = sem("ctx_rest")
        wv_hi_made, wv_lo_made = sem("wv_hi_made"), sem("wv_lo_made")
        a_done, a_hi_made, a_lo_made = sem("a_done"), sem("a_hi_made"), sem("a_lo_made")
        ln1_stats, ln1_aggr, ln1_eps, ln1_rstd = sem("ln1_stats"), sem("ln1_aggr"), sem("ln1_eps"), sem("ln1_rstd")
        xn_made, xT_done, xT_hi_made, xT_lo_made = sem("xn_made"), sem("xT_done"), sem("xT_hi_made"), sem("xT_lo_made")
        xbo_made = sem("xbo_made")
        proj_done, t_hi_made, t_lo_made = sem("proj_done"), sem("t_hi_made"), sem("t_lo_made")
        v_done, v_kept = sem("v_done"), sem("v_kept")
        scored, maxed, exped = sem("scored"), sem("maxed"), sem("exped")
        rden_made, normed, transposed = sem("rden_made"), sem("normed"), sem("transposed")
        ptr_kept = sem("ptr_kept")
        pv_done, attn_kept, wo_done = sem("pv_done"), sem("attn_kept"), sem("wo_done")
        ln2_stats, ln2_aggr, ln2_eps, ln2_rstd = (sem(s) for s in ("ln2_stats", "ln2_aggr", "ln2_eps", "ln2_rstd"))
        t_made, tb2_made = sem("t_made"), sem("tb2_made")
        ffn_done = sem("ffn_done")
        ffn_kept = sem("ffn_kept")
        y_made, ln3_stats, ln3_aggr, ln3_eps, ln3_rstd = (sem(s) for s in ("y_made", "ln3_stats", "ln3_aggr", "ln3_eps", "ln3_rstd"))
        wo_kept = sem("wo_kept")
        x2b_made, yg_made = sem("x2b_made"), sem("yg_made")
        out_made, stored = sem("out_made"), sem("stored")
        tail_hid = sem("tail_hid")
        tail_relu = [sem("tail_relu_act"), sem("tail_relu_dve")]

        def cols(b, n):
            return slice(b * n, b * n + n) if isinstance(b, int) else bass.ds(b * n, n)

        def after(b):
            return nc.s_assert_within(b + 1, 1, B - 1,
                                      skip_runtime_bounds_check_because="used only where b < B - 1")

        def before(b):
            return (b * (B - 1)) // B

        def when(eng, holds, cond, emit):
            if holds:
                emit()
            else:
                with eng.If(cond()):
                    emit()

        block = ctx.enter_context(nc.Block())

        @block.sync
        def _(sp):
            sp.dma_start(x_sb[:, :, :], x.rearrange("(t p) d -> p t d", p=P)).then_inc(ld_x, 16)
            sp.dma_start(wv_sb[:, :], Wv).then_inc(ld_wv, 16)
            for k, row in enumerate((bo, b2, gamma, beta)):
                sp.dma_start(rows[:, k, :], row.partition_broadcast(P)).then_inc(ld_rows, 16)
            sp.dma_start(wo_sb[:, :, :], Wo.rearrange("(q p) d -> p q d", p=P)).then_inc(ld_wo, 16)
            sp.dma_start(w1_sb[:, :], w1).then_inc(ld_ffn, 16)
            sp.dma_start(w2_sb[:, :, :], w2.rearrange("(c p) d -> p c d", p=P)).then_inc(ld_ffn, 16)
            sp.dma_start(b1_sb[:, :], b1T).then_inc(ld_ffn, 16)

            def move_context(half, bb):
                for dst, src in ((cv_hi[half], ctx_hi), (cv_lo[half], ctx_lo)):
                    sp.dma_start(dst[:, :].bitcast(F32), src[:, cols(bb, NK)].bitcast(F32)).then_inc(ld_cv[half], 16)

            sp.wait_ge(ctx_hi_made, 1)
            sp.wait_ge(ctx_lo_made, 1)
            move_context(1, 0)
            with sp.Fori(0, B) as b:
                with sp.If(b < B - 1):
                    sp.wait_ge(ctx_rest, b * 2 + 2)
                    sp.wait_ge(v_done, b * 8 + 4)
                    move_context(0, after(b))
                    sp.wait_ge(v_done, b * 8 + 8)
                    move_context(1, after(b))
                with sp.If(b > 0):
                    sp.wait_ge(out_made, b * TT + 1)
                    sp.dma_start(out[cols(before(b), NQ), :].rearrange("(t p) d -> p t d", p=P),
                                 out_sb[:, cols(before(b), TT), :]).then_inc(stored, 16)
            for t in range((B - 1) * TT, NT):
                sp.wait_ge(out_made, t + 2)
                sp.dma_start(out[t * P:t * P + P, :], out_sb[:, t, :]).then_inc(stored, 16)
            sp.wait_ge(stored, 16 * (B - 1 + TT))

        @block.gpsimd
        def _(pool):
            nc.gpsimd.memset(ident[:, :], 0.0).then_inc(consts_made, 1)
            nc.gpsimd.memset(neghalf[:, :], -0.5).then_inc(consts_made, 1)
            nc.gpsimd.memset(eps[:, :], EPS).then_inc(consts_made, 1)
            pool.wait_ge(consts_made, 3)
            nc.gpsimd.affine_select(out=ident[:, :], in_=ident[:, :], compare_op=ALU.not_equal, fill=1.0,
                                    base=0, pattern=[[-1, P]], channel_multiplier=1).then_inc(consts_made, 1)
            for g in range(NT // GT):
                tiles = slice(g * GT, g * GT + GT)
                pool.wait_ge(ln1_aggr, g * GT + GT)
                nc.gpsimd.tensor_tensor(ve1[:, tiles], mv1[:, tiles, 1], eps[:, :], ALU.add).then_inc(ln1_eps, 1)
                pool.wait_ge(ln1_eps, g + 1)
                nc.gpsimd.tensor_tensor(rs1[:, tiles], ve1[:, tiles], neghalf[:, :], ALU.pow).then_inc(ln1_rstd, 1)
            pool.wait_ge(ld_ctx, 16)
            for b in range(1, B):
                c = cols(b, NK)
                nc.gpsimd.tensor_copy(ctx_hi[:, c], ctx_sb[:, c]).then_inc(ctx_rest, 1)
                pool.wait_ge(ctx_rest, 2 * b - 1)
                nc.gpsimd.tensor_tensor(ctx_lo[:, c], ctx_sb[:, c], ctx_hi[:, c].bitcast(F32),
                                        ALU.subtract).then_inc(ctx_rest, 1)
            pool.wait_ge(ld_rows, 4 * 16)
            pool.wait_ge(ld_x, 16)
            nc.gpsimd.tensor_tensor(xbo[:, :, :], x_sb[:, :, :],
                                    bo_b.unsqueeze(1).to_broadcast([P, NT, D]), ALU.add).then_inc(xbo_made, 1)

            def per_tile(row):
                return row.unsqueeze(1).to_broadcast([P, TT, D])

            with pool.Fori(0, B) as b:
                pool.wait_ge(ln2_aggr, b * TT + TT)
                nc.gpsimd.tensor_tensor(ve2[:, :], mv2[:, :, 1], eps[:, 0:TT], ALU.add).then_inc(ln2_eps, 1)
                pool.wait_ge(ln2_eps, b + 1)
                nc.gpsimd.tensor_tensor(rs2[:, :], ve2[:, :], neghalf[:, 0:TT], ALU.pow).then_inc(ln2_rstd, 1)
                nc.gpsimd.tensor_tensor(x2b[:, :, :], x2[:, :, :], per_tile(beta_b), ALU.add).then_inc(x2b_made, 1)
                pool.wait_ge(t_made, b * TT + TT)
                nc.gpsimd.tensor_tensor(tb2[:, :, :], t_sb[:, :, :], per_tile(b2_b), ALU.add).then_inc(tb2_made, 1)
                pool.wait_ge(ln3_aggr, b * TT + TT)
                nc.gpsimd.tensor_tensor(ve3[:, :], mv3[:, :, 1], eps[:, 0:TT], ALU.add).then_inc(ln3_eps, 1)
                pool.wait_ge(ln3_eps, b + 1)
                nc.gpsimd.tensor_tensor(rs3[:, :], ve3[:, :], neghalf[:, 0:TT], ALU.pow).then_inc(ln3_rstd, 1)

        @block.scalar
        def _(act):
            act.dma_start(wqT_sb[:, :, :], WqT).then_inc(ld_wqk, 16)
            act.dma_start(wkT_sb[:, :, :], WkT).then_inc(ld_wqk, 16)
            act.dma_start(ctx_sb[:, :], ctxT).then_inc(ld_ctx, 16)

            def keep_a_hi(g):
                act.wait_ge(a_done, g + 1)
                nc.scalar.activation(a_hi[:, GH * g:GH * g + GH, :].rearrange("d h c -> d (h c)"),
                                     score_bank[g][:, 0:GH * C], ACT.Copy, scale=SCALE).then_inc(a_hi_made, 1)

            def keep_xT_hi(g, src):
                act.wait_ge(xT_done, g + 1)
                nc.scalar.activation(xnT_hi[:, 512 * g:512 * g + 512], src[:, :], ACT.Copy).then_inc(xT_hi_made, 1)

            def keep_t_hi(u, par):
                act.wait_ge(proj_done, u + 1)
                nc.scalar.activation(t_hi[:, par, :], proj_bank[0:C, :], ACT.Copy).then_inc(t_hi_made, 1)

            def keep_values(n, half, kt):
                act.wait_ge(v_done, n + 1)
                nc.scalar.activation(values[:, kt, half * HALF:half * HALF + HALF], proj_bank[:, :],
                                     ACT.Copy).then_inc(v_kept, 1)

            def exp_tile(n, par, i):
                act.wait_ge(maxed, n + 1)
                nc.scalar.activation(probs[:, i, :], score_bank[i][:, :], ACT.Exp, bias=negmax[:, par, i:i + 1],
                                     accum_out=den[:, par, i:i + 1]).then_inc(exped, 1)

            def keep_transposed(n, par, i):
                h, qt = i // QT, i % QT
                act.wait_ge(transposed, n + 1)
                nc.scalar.activation(probsT[:, par, h, :, qt * P:qt * P + P],
                                     ptr_bank[:, :].rearrange("k (t q) -> k t q", t=KT),
                                     ACT.Copy).then_inc(ptr_kept, 1)

            def keep_tT(fb):
                act.wait_ge(ffn_done, fb * 4 + 1)
                nc.scalar.activation(tT[:, :], pv_bank[:, 0:NQ], ACT.Copy).then_inc(ffn_kept, 1)

            def keep_hidden(fb, k):
                act.wait_ge(ffn_done, fb * 4 + 2 + k)
                for j in range(2):
                    c = 2 * k + j
                    ins = nc.scalar.activation(hid[:, c, :], pv_bank[:, j * NQ:j * NQ + NQ], ACT.Relu,
                                               bias=b1_sb[:, c:c + 1])
                ins.then_inc(ffn_kept, 1)

            act.wait_ge(ld_ctx, 16)
            nc.scalar.activation(ctx_hi[:, 0:NK], ctx_sb[:, 0:NK], ACT.Copy).then_inc(ctx_hi_made, 1)
            act.wait_ge(ld_wv, 16)
            for half in range(2):
                c = slice(half * HALF, half * HALF + HALF)
                nc.scalar.activation(wv_hi[:, c], wv_sb[:, c], ACT.Copy).then_inc(wv_hi_made, 1)
            keep_a_hi(0)
            keep_xT_hi(0, ptr_bank)
            for g in range(1, H // GH):
                keep_a_hi(g)
            keep_t_hi(0, 0)
            keep_xT_hi(1, pv_bank)
            keep_values(0, 0, 0)
            keep_t_hi(1, 1)
            keep_values(1, 0, 1)
            exp_tile(0, 0, 0)
            exp_tile(1, 0, 1)
            keep_values(2, 0, 2)
            exp_tile(2, 0, 2)
            exp_tile(3, 0, 3)
            keep_values(3, 0, 3)
            act.wait_ge(ld_ffn, 3 * 16)

            with act.Fori(0, B) as b:
                for p in range(PAIRS):
                    par, nxt = p % 2, (p + 1) % 2
                    n = b * (4 * PAIRS) + 4 * p
                    for i in range(4):
                        keep_transposed(n + i, par, i)
                        when(act, p < PAIRS - 1, lambda: b < B - 1, lambda: exp_tile(n + 4 + i, nxt, i))
                        if i == 1:
                            when(act, p < PAIRS - 2, lambda: b < B - 1,
                                 lambda: keep_t_hi(b * PAIRS + p + 2, par))
                    if p == 3:
                        when(act, False, lambda: b > 0, lambda: keep_tT(before(b)))
                    if p in (4, 5):
                        when(act, False, lambda: b > 0, lambda: keep_hidden(before(b), p - 4))
                    when(act, p < 4, lambda: b < B - 1,
                         lambda: keep_values(b * 8 + 4 + p, 1 if p < 4 else 0, p % 4))
            keep_tT(B - 1)
            for c in range(0, FC, 2):
                act.wait_ge(tail_hid, c + 1)
                nc.scalar.activation(hid[:, c, :], score_bank[c][:, 0:NQ], ACT.Relu,
                                     bias=b1_sb[:, c:c + 1]).then_inc(tail_relu[0], 1)

        @block.vector
        def _(dve):
            def stats(st, mv, src, tiles, s_stats, s_aggr, base, carrier=None):
                for k, t in enumerate(tiles):
                    nc.vector.bn_stats(st[:, t, :], src[:, t, :]).then_inc(s_stats, 1)
                for k, t in enumerate(tiles):
                    if isinstance(base, int):
                        dve.wait_ge(s_stats, base + k + 1)
                    elif k == 0:
                        dve.wait_ge(s_stats, base + len(tiles))
                        nc.vector.memset(carrier[:, :], 0.0)
                    nc.vector.bn_aggr(mv[:, t, :], st[:, t, :]).then_inc(s_aggr, 1)

            def apply_norm(dst, src, mv, rs, t, s_made):
                nc.vector.tensor_scalar(dst[:, t, :], src[:, t, :], mv[:, t, 0:1], rs[:, t:t + 1],
                                        ALU.subtract, ALU.mult).then_inc(s_made, 1)

            def low_half(lo, full, hi, s_made):
                nc.vector.tensor_tensor(lo, full, hi.bitcast(F32), ALU.subtract).then_inc(s_made, 1)

            def keep_a_lo(g):
                heads = slice(GH * g, GH * g + GH)
                dve.wait_ge(a_hi_made, g + 1)
                nc.vector.scalar_tensor_tensor(out=a_lo[:, heads, :].rearrange("d h c -> d (h c)"),
                                               in0=score_bank[g][:, 0:GH * C], scalar=SCALE,
                                               in1=a_hi[:, heads, :].rearrange("d h c -> d (h c)").bitcast(F32),
                                               op0=ALU.mult, op1=ALU.subtract).then_inc(a_lo_made, 1)

            def keep_xT_lo(g, src):
                c = slice(512 * g, 512 * g + 512)
                dve.wait_ge(xT_hi_made, g + 1)
                low_half(xnT_lo[:, c], src[:, :], xnT_hi[:, c], xT_lo_made)

            def keep_t_lo(u, par):
                dve.wait_ge(t_hi_made, u + 1)
                low_half(t_lo[:, par, :], proj_bank[0:C, :], t_hi[:, par, :], t_lo_made)

            def row_max(n, par, i):
                dve.wait_ge(scored, n + 1)
                nc.vector.tensor_reduce(negmax[:, par, i:i + 1], score_bank[i][:, :], AX_X, ALU.max,
                                        negate=True).then_inc(maxed, 1)

            def row_rden(n, par, i):
                dve.wait_ge(exped, n + 1)
                nc.vector.reciprocal(rden[:, par, i:i + 1], den[:, par, i:i + 1]).then_inc(rden_made, 1)

            def row_norm(n, par, i):
                dve.wait_ge(rden_made, n + 1)
                nc.vector.tensor_scalar(probs[:, i, :], probs[:, i, :], rden[:, par, i:i + 1], None,
                                        ALU.mult).then_inc(normed, 1)

            def keep_attn(u, par):
                dve.wait_ge(pv_done, u + 1)
                nc.vector.tensor_copy(attnT[:, par, :], pv_bank[:, 0:NQ]).then_inc(attn_kept, 1)

            def residual(fb):
                dve.wait_ge(wo_done, fb * PAIRS + PAIRS)
                dve.wait_ge(xbo_made, 1)
                dve.wait_ge(out_made, fb * TT + 1)
                xr = xbo[:, 2 * fb:2 * fb + TT, :] if isinstance(fb, int) else xbo[:, bass.ds(fb * TT, TT), :]
                nc.vector.tensor_tensor(x2[:, :, :], wo_bank[:, 0:NQ].rearrange("p (t d) -> p t d", t=TT), xr,
                                        ALU.add).then_inc(wo_kept, 1)
                dve.wait_ge(wo_kept, fb + 2)
                stats(st2, mv2, x2, range(TT), ln2_stats, ln2_aggr, fb * TT, carrier2)

            def norm2(fb):
                dve.wait_ge(ln2_rstd, fb + 1)
                for t in range(TT):
                    apply_norm(t_sb, x2, mv2, rs2, t, t_made)

            def finish_y(fb, done, kept):
                dve.wait_ge(ffn_done, done)
                dve.wait_ge(tb2_made, fb + 1)
                nc.vector.tensor_tensor(y_sb[:, :, :], pv_bank[:, 0:NQ].rearrange("p (t d) -> p t d", t=TT),
                                        tb2[:, :, :], ALU.add).then_inc(ffn_kept, 1)
                dve.wait_ge(ffn_kept, kept)
                stats(st3, mv3, y_sb, range(TT), ln3_stats, ln3_aggr, fb * TT, carrier3)

            def last_sum(fb):
                dve.wait_ge(ln3_rstd, fb + 1)
                for t in range(TT):
                    nc.vector.scalar_tensor_tensor(out=yg[:, t, :], in0=y_sb[:, t, :], scalar=mv3[:, t, 0:1],
                                                   in1=gamma_b, op0=ALU.subtract, op1=ALU.mult).then_inc(yg_made, 1)
                dve.wait_ge(x2b_made, fb + 1)
                for t in range(TT):
                    dve.wait_ge(yg_made, fb * TT + t + 1)
                    o = out_sb[:, fb * TT + t, :] if isinstance(fb, int) else \
                        out_sb[:, bass.ds(fb * TT + t, 1), :].rearrange("p t d -> p (t d)")
                    nc.vector.scalar_tensor_tensor(out=o, in0=yg[:, t, :], scalar=rs3[:, t:t + 1],
                                                   in1=x2b[:, t, :], op0=ALU.mult, op1=ALU.add).then_inc(out_made, 1)

            nc.vector.memset(credits[:, 0:1], 0.0).then_inc(ffn_kept, 4)
            nc.vector.memset(credits[:, 1:2], 0.0).then_inc(wo_kept, 1)
            nc.vector.memset(credits[:, 2:3], 0.0).then_inc(out_made, 1)

            dve.wait_ge(ld_x, 16)
            stats(st1, mv1, x_sb, range(0, GT), ln1_stats, ln1_aggr, 0)
            stats(st1, mv1, x_sb, range(GT, NT), ln1_stats, ln1_aggr, GT)
            dve.wait_ge(ctx_hi_made, 1)
            low_half(ctx_lo[:, 0:NK], ctx_sb[:, 0:NK], ctx_hi[:, 0:NK], ctx_lo_made)
            dve.wait_ge(ln1_rstd, 1)
            for t in range(GT):
                apply_norm(xn, x_sb, mv1, rs1, t, xn_made)
            for half in range(2):
                c = slice(half * HALF, half * HALF + HALF)
                dve.wait_ge(wv_hi_made, half + 1)
                low_half(wv_lo[:, c], wv_sb[:, c], wv_hi[:, c], wv_lo_made)
            keep_a_lo(0)
            keep_xT_lo(0, ptr_bank)
            dve.wait_ge(xT_lo_made, 1)
            nc.vector.memset(credits[:, 3:4], 0.0).then_inc(ptr_kept, 1)
            for g in range(1, H // GH):
                keep_a_lo(g)
            keep_t_lo(0, 0)
            dve.wait_ge(ln1_rstd, 2)
            for t in range(GT, NT):
                apply_norm(xn, x_sb, mv1, rs1, t, xn_made)
            keep_xT_lo(1, pv_bank)
            keep_t_lo(1, 1)
            for i in range(4):
                row_max(i, 0, i)
                if i:
                    row_rden(i - 1, 0, i - 1)
                    row_norm(i - 1, 0, i - 1)

            with dve.Fori(0, B) as b:
                for p in range(PAIRS):
                    par, nxt = p % 2, (p + 1) % 2
                    n = b * (4 * PAIRS) + 4 * p
                    for i in range(4):
                        if i == 0:
                            row_rden(n + 3, par, 3)
                        if i == 3:
                            when(dve, p > 0, lambda: b > 0, lambda: keep_attn(b * PAIRS + p - 1, nxt))

                        def scores_part():
                            if i:
                                row_rden(n + 4 + i - 1, nxt, i - 1)
                            row_max(n + 4 + i, nxt, i)
                            if i:
                                row_norm(n + 4 + i - 1, nxt, i - 1)
                        when(dve, p < PAIRS - 1, lambda: b < B - 1, scores_part)
                        if i == 0:
                            row_norm(n + 3, par, 3)
                            if p == 1:
                                when(dve, False, lambda: b > 0, lambda: residual(before(b)))
                            if p == 2:
                                when(dve, False, lambda: b > 0, lambda: norm2(before(b)))
                            if p == 7:
                                when(dve, False, lambda: b > 0,
                                     lambda: finish_y(before(b), before(b) * 4 + 4, before(b) * 4 + 8))
                        if i == 2:
                            when(dve, p < PAIRS - 2, lambda: b < B - 1,
                                 lambda: keep_t_lo(b * PAIRS + p + 2, par))
                    if p == 7:
                        when(dve, False, lambda: b > 0, lambda: last_sum(before(b)))
            keep_attn(UNITS - 1, 1)
            residual(B - 1)
            norm2(B - 1)
            for c in range(1, FC, 2):
                dve.wait_ge(tail_hid, c + 1)
                nc.vector.tensor_scalar(hid[:, c, :], score_bank[c][:, 0:NQ], b1_sb[:, c:c + 1], 0.0,
                                        ALU.add, ALU.max).then_inc(tail_relu[1], 1)
            finish_y(B - 1, (B - 1) * 4 + 2, B * 4 + 2)
            last_sum(B - 1)

        @block.tensor
        def _(pe):
            def three(dst, w, m, start=True):
                (w_hi, w_lo), (m_hi, m_lo) = w, m
                nc.tensor.matmul(dst, w_hi, m_hi, start=start, stop=False)
                nc.tensor.matmul(dst, w_hi, m_lo, start=False, stop=False)
                return nc.tensor.matmul(dst, w_lo, m_hi, start=False, stop=True)

            def make_a(g):
                for j in range(GH):
                    h = GH * g + j
                    ins = nc.tensor.matmul(score_bank[g][:, j * C:j * C + C], wqT_sb[:, h, :], wkT_sb[:, h, :],
                                           start=True, stop=True)
                ins.then_inc(a_done, 1)

            def transpose_x(g, dst):
                pe.wait_ge(xn_made, GT * g + GT)
                for j in range(GT):
                    ins = nc.tensor.transpose(dst[:, j * P:j * P + P], xn[:, GT * g + j, :], ident[:, :])
                ins.then_inc(xT_done, 1)

            def project(p, bb):
                for h in range(2):
                    hh = 2 * p + h
                    ins = three(proj_bank[0:C, h * NQ:h * NQ + NQ], (a_hi[:, hh, :], a_lo[:, hh, :]),
                                (xnT_hi[:, cols(bb, NQ)], xnT_lo[:, cols(bb, NQ)]))
                ins.then_inc(proj_done, 1)

            def value_piece(chi, clo, half, kt):
                k, c = slice(kt * P, kt * P + P), slice(half * HALF, half * HALF + HALF)
                three(proj_bank[:, :], (chi[:, k], clo[:, k]), (wv_hi[:, c], wv_lo[:, c])).then_inc(v_done, 1)

            def score(par, i, bb):
                h, qt = i // QT, i % QT
                q = slice(h * NQ + qt * P, h * NQ + qt * P + P)
                three(score_bank[i][:, :], (t_hi[:, par, q], t_lo[:, par, q]),
                      (ctx_hi[:, cols(bb, NK)], ctx_lo[:, cols(bb, NK)])).then_inc(scored, 1)

            def transpose_probs(i):
                for kt in range(KT):
                    ins = nc.tensor.transpose(ptr_bank[:, kt * P:kt * P + P], probs[:, i, kt * P:kt * P + P],
                                              ident[:, :])
                ins.then_inc(transposed, 1)

            def times_values(p, par, key_tiles):
                for kt in key_tiles:
                    for h in range(2):
                        c = (2 * p + h) * DH
                        ins = nc.tensor.matmul(pv_bank[h * DH:h * DH + DH, 0:NQ], values[:, kt, c:c + DH],
                                               probsT[:, par, h, kt, :], start=(kt == 0), stop=(kt == KT - 1))
                if kt == KT - 1:
                    ins.then_inc(pv_done, 1)

            def out_project(p, par):
                for t in range(TT):
                    ins = nc.tensor.matmul(wo_bank[:, t * D:t * D + D], attnT[:, par, t * P:t * P + P],
                                           wo_sb[:, p, :], start=(p == 0 and t == 0), stop=(p == PAIRS - 1),
                                           skip_group_check=True)
                ins.then_inc(wo_done, 1)

            def ffn_piece(k, fb):
                if k == 0:
                    pe.wait_ge(t_made, fb * TT + TT)
                    for t in range(TT):
                        ins = nc.tensor.transpose(pv_bank[:, t * P:t * P + P], t_sb[:, t, :], ident[:, :])
                elif k < 3:
                    pe.wait_ge(ffn_kept, fb * 4 + 4 + k)
                    for j in range(2):
                        c = 2 * (k - 1) + j
                        ins = nc.tensor.matmul(pv_bank[:, j * NQ:j * NQ + NQ], w1_sb[:, c * P:c * P + P], tT[:, :],
                                               start=True, stop=True)
                else:
                    pe.wait_ge(ffn_kept, fb * 4 + 4 + 3)
                    for t in range(TT):
                        for c in range(FC):
                            ins = nc.tensor.matmul(pv_bank[:, t * D:t * D + D], hid[:, c, t * P:t * P + P],
                                                   w2_sb[:, c, :], start=(c == 0), stop=(c == FC - 1))
                ins.then_inc(ffn_done, 1)

            pe.wait_ge(ld_wqk, 32)
            for g in range(H // GH):
                make_a(g)
            pe.wait_ge(consts_made, 4)
            transpose_x(0, ptr_bank)
            pe.wait_ge(a_lo_made, 1)
            pe.wait_ge(xT_lo_made, 1)
            project(0, 0)
            transpose_x(1, pv_bank)
            pe.wait_ge(ctx_lo_made, 1)
            pe.wait_ge(wv_lo_made, 2)
            pe.wait_ge(t_lo_made, 1)
            value_piece(ctx_hi, ctx_lo, 0, 0)
            pe.wait_ge(v_kept, 1)
            project(1, 0)
            pe.wait_ge(t_lo_made, 2)
            value_piece(ctx_hi, ctx_lo, 0, 1)
            pe.wait_ge(a_lo_made, 4)
            score(0, 0, 0)
            score(0, 1, 0)
            pe.wait_ge(v_kept, 2)
            value_piece(ctx_hi, ctx_lo, 0, 2)
            score(0, 2, 0)
            score(0, 3, 0)
            pe.wait_ge(v_kept, 3)
            value_piece(ctx_hi, ctx_lo, 0, 3)
            pe.wait_ge(xT_lo_made, 2)
            pe.wait_ge(ld_wo, 16)
            pe.wait_ge(ld_ffn, 3 * 16)

            with pe.Fori(0, B) as b:
                for p in range(PAIRS):
                    par, nxt = p % 2, (p + 1) % 2
                    u = b * PAIRS + p
                    n = b * (4 * PAIRS) + 4 * p
                    for i in range(4):
                        def next_score():
                            pe.wait_ge(exped, n + i + 1)
                            if i == 0:
                                pe.wait_ge(t_lo_made, u + 2)
                                if p == PAIRS - 1:
                                    pe.wait_ge(ctx_rest, b * 2 + 2)
                            score(nxt, i, after(b) if p == PAIRS - 1 else b)
                        when(pe, p < PAIRS - 1, lambda: b < B - 1, next_score)

                        pe.wait_ge(normed, n + i + 1)
                        pe.wait_ge(ptr_kept, n + i + 1)
                        transpose_probs(i)

                        if i == 0:
                            def prev_values():
                                if p in (1, 5):
                                    pe.wait_ge(v_kept, b * 8 + 4 + p - 1)
                                if p >= 4:
                                    pe.wait_ge(ffn_kept, b * 4 + p - 3)
                                times_values((p - 1) % PAIRS, nxt, range(0, KT // 2))
                            when(pe, p > 0, lambda: b > 0, prev_values)
                        if i == 1:
                            def next_project():
                                if p == 5:
                                    with pe.If(b < B - 1):
                                        pe.wait_ge(v_kept, b * 8 + 4 + p)
                                else:
                                    pe.wait_ge(v_kept, b * 8 + 4 + p)
                                project((p + 2) % PAIRS, b if p < PAIRS - 2 else after(b))
                            when(pe, p < PAIRS - 2, lambda: b < B - 1, next_project)
                        if i == 2:
                            when(pe, p > 0, lambda: b > 0,
                                 lambda: times_values((p - 1) % PAIRS, nxt, range(KT // 2, KT)))
                        if i == 3:
                            def prev_project():
                                pe.wait_ge(attn_kept, u)
                                if p == 1:
                                    pe.wait_ge(wo_kept, b + 1)
                                out_project((p - 1) % PAIRS, nxt)
                            when(pe, p > 0, lambda: b > 0, prev_project)
                            if 3 <= p <= 6:
                                when(pe, False, lambda: b > 0, lambda: ffn_piece(p - 3, before(b)))

                            def next_value_piece():
                                pe.wait_ge(t_lo_made, u + 3)
                                half = 1 if p < 4 else 0
                                pe.wait_ge(ld_cv[half], (b + 1) * 32)
                                value_piece(cv_hi[half], cv_lo[half], half, p % 4)
                            when(pe, p < 4, lambda: b < B - 1, next_value_piece)
            pe.wait_ge(ptr_kept, UNITS * 4 + 1)
            times_values(PAIRS - 1, 1, range(KT))
            pe.wait_ge(attn_kept, UNITS)
            out_project(PAIRS - 1, 1)
            ffn_piece(0, B - 1)
            pe.wait_ge(ffn_kept, B * 4 + 1)
            for c in range(FC):
                nc.tensor.matmul(score_bank[c][:, 0:NQ], w1_sb[:, c * P:c * P + P], tT[:, :],
                                 start=True, stop=True).then_inc(tail_hid, 1)
            for c in range(FC):
                pe.wait_ge(tail_relu[c % 2], c // 2 + 1)
                for t in range(TT):
                    ins = nc.tensor.matmul(pv_bank[:, t * D:t * D + D], hid[:, c, t * P:t * P + P], w2_sb[:, c, :],
                                           start=(c == 0 and t == 0), stop=(c == FC - 1), skip_group_check=True)
            ins.then_inc(ffn_done, 1)


def kernel(x, ctx_768, L0_xattn_Wq, L0_xattn_Wk, L0_xattn_Wv, L0_xattn_Wo, L0_xattn_bo,
           L0_ffn_router_w, L0_ffn_router_b, L0_ffn_w1, L0_ffn_b1, L0_ffn_w2, L0_ffn_b2,
           L0_ffn_gamma, L0_ffn_beta):
    import numpy as np
    import concourse.bacc as bacc
    from concourse.bass_utils import run_bass_kernel_spmd

    B, NQ, D = x.shape
    C = ctx_768.shape[2]
    H, DH, P = 16, 64, 128
    Wq, Wk = np.asarray(L0_xattn_Wq), np.asarray(L0_xattn_Wk)
    arrays = {
        "x": np.asarray(x).reshape(B * NQ, D),
        "ctxT": np.asarray(ctx_768).transpose(2, 0, 1).reshape(C, -1),
        "WqT": Wq.reshape(D, H, DH).transpose(2, 1, 0),
        "WkT": Wk.reshape(C, H, DH).transpose(2, 1, 0),
        "Wv": np.asarray(L0_xattn_Wv),
        "Wo": np.asarray(L0_xattn_Wo),
        "bo": np.asarray(L0_xattn_bo),
        "w1": np.asarray(L0_ffn_w1)[0],
        "b1T": np.asarray(L0_ffn_b1)[0].reshape(-1, P).T,
        "w2": np.asarray(L0_ffn_w2)[0],
        "b2": np.asarray(L0_ffn_b2)[0],
        "gamma": np.asarray(L0_ffn_gamma),
        "beta": np.asarray(L0_ffn_beta),
    }
    arrays = {f"in_{k}": np.ascontiguousarray(v) for k, v in arrays.items()}
    nc = bacc.Bacc("TRN2", target_bir_lowering=False, num_devices=1)
    args = [nc.dram_tensor(k, v.shape, mybir.dt.from_np(v.dtype), kind="ExternalInput").ap()
            for k, v in arrays.items()]
    args.append(nc.dram_tensor("out", (B * NQ, D), F32, kind="ExternalOutput").ap())
    xattn_ffn_kernel(nc, *args)
    r = run_bass_kernel_spmd(nc, [arrays], core_ids=[0])
    return r.results[0]["out"].reshape(B, NQ, D)
```

```python
from contextlib import ExitStack

import concourse.bass as bass
from concourse import mybir

ALU = mybir.AluOpType
ACT = mybir.ActivationFunctionType
F32 = mybir.dt.float32
F32R = mybir.dt.float32r
AX_X = mybir.AxisListType.X
EPS = 1e-5


def xattn_ffn_kernel(nc, x, ctxT, Wq, Wk, Wv, Wo, bo, w1, b1T, w2, b2, gamma, beta, out):
    P = 128
    N, D = x.shape
    C, NKB = ctxT.shape
    INNER = Wq.shape[1]
    DH = 64
    H = INNER // DH
    F = w1.shape[1]
    B = 4
    NQ, NK = N // B, NKB // B
    PAIRS = H // 2
    UNITS = B * PAIRS
    QT, KT, TT = NQ // P, NK // P, NQ // P
    NT = N // P
    FC = F // P
    LN_GROUPS = ((0, TT), (TT, NT))
    XT_GROUPS = ((0, TT), (TT, 6), (6, NT))
    HALF = INNER // 2
    SCALE = DH ** -0.5
    assert D == P and NK == 512 and QT == 2 and KT == 4 and FC == 4 and PAIRS == 8 and C <= P

    with ExitStack() as ctx:
        def sb(name, shape, dt=F32):
            return ctx.enter_context(nc.sbuf_tensor(name, shape, dt))

        def bank(name):
            return ctx.enter_context(nc.psum_tensor(name, [P, 512], F32))

        def sem(name):
            return ctx.enter_context(nc.semaphore(name))

        x_sb = sb("x_sb", [P, NT, D])
        wq_sb = sb("wq_sb", [D, INNER])
        wk_sb = sb("wk_sb", [C, INNER])
        ctx_sb = sb("ctx_sb", [C, NKB])
        wv_sb = sb("wv_sb", [C, INNER])
        wo_sb = sb("wo_sb", [P, PAIRS, D])
        w1_sb = sb("w1_sb", [D, F])
        w2_sb = sb("w2_sb", [P, FC, D])
        b1_sb = sb("b1_sb", [P, FC])
        rows = sb("rows", [P, 4, D])
        bo_b, b2_b, gamma_b, beta_b = (rows[:, k, :] for k in range(4))

        ctx_hi, ctx_lo = sb("ctx_hi", [C, NKB], F32R), sb("ctx_lo", [C, NKB], F32R)
        wv_hi, wv_lo = sb("wv_hi", [C, INNER], F32R), sb("wv_lo", [C, INNER], F32R)
        wq_hi, wq_lo = sb("wq_hi", [D, INNER], F32R), sb("wq_lo", [D, INNER], F32R)
        wk_hi, wk_lo = sb("wk_hi", [C, INNER], F32R), sb("wk_lo", [C, INNER], F32R)
        xnT_hi, xnT_lo = sb("xnT_hi", [D, N], F32R), sb("xnT_lo", [D, N], F32R)
        q_hh = sb("q_hh", [P, 2, 2, NQ], F32R)
        k_hl = sb("k_hl", [P, 2, 2, NK], F32R)
        q_lo = sb("q_lo", [P, 2, NQ], F32R)
        cv_hi = [sb(f"cv_hi{h}", [C, NK], F32R) for h in range(2)]
        cv_lo = [sb(f"cv_lo{h}", [C, NK], F32R) for h in range(2)]

        ident = sb("ident", [P, P])
        xn = sb("xn", [P, NT, D])
        values = sb("values", [P, KT, INNER])
        probs = sb("probs", [P, 4, NK])
        probsT = sb("probsT", [P, 2, 2, KT, NQ])
        negmax = sb("negmax", [P, 2, 4])
        den = sb("den", [P, 2, 4])
        rden = sb("rden", [P, 2, 4])
        attnT = sb("attnT", [P, 2, NQ])

        neghalf, eps = sb("neghalf", [P, NT]), sb("eps", [P, NT])
        st1, mv1 = sb("st1", [P, NT, 6]), sb("mv1", [P, NT, 2])
        ve1, rs1 = sb("ve1", [P, NT]), sb("rs1", [P, NT])
        st2, mv2 = sb("st2", [P, TT, 6]), sb("mv2", [P, TT, 2])
        ve2, rs2 = sb("ve2", [P, TT]), sb("rs2", [P, TT])
        st3, mv3 = sb("st3", [P, TT, 6]), sb("mv3", [P, TT, 2])
        ve3, rs3 = sb("ve3", [P, TT]), sb("rs3", [P, TT])
        carrier2, carrier3 = sb("carrier2", [P, 1]), sb("carrier3", [P, 1])
        credits = sb("credits", [P, 4])
        xbo = sb("xbo", [P, NT, D])
        x2 = sb("x2", [P, TT, D])
        x2b = sb("x2b", [P, TT, D])
        t_sb = sb("t_sb", [P, TT, D])
        tb2 = sb("tb2", [P, TT, D])
        tT = sb("tT", [D, NQ])
        hid = sb("hid", [P, FC, NQ])
        y_sb = sb("y_sb", [P, TT, D])
        t_cent, y_cent, y_norm = (sb(s, [P, TT, D]) for s in ("t_cent", "y_cent", "y_norm"))
        xn_cent = sb("xn_cent", [P, NT - TT, D])
        yg = sb("yg", [P, TT, D])
        out_sb = sb("out_sb", [P, NT, D])

        score_bank = [bank(f"score_bank{i}") for i in range(2)]
        ptr_bank = bank("ptr_bank")
        pv_bank = bank("pv_bank")
        q_bank, k_bank = bank("q_bank"), bank("k_bank")
        v_bank = bank("v_bank")
        last_ptr = (q_bank, k_bank, ptr_bank, score_bank[0])
        tail_pv_bank, tail_tT_bank, tail_y_bank = (score_bank[1], pv_bank), (v_bank, pv_bank), (v_bank, score_bank[1])
        tail_hid_bank = ((q_bank, k_bank), (ptr_bank, score_bank[0]))
        wo_bank = bank("wo_bank")

        ld_x0, ld_x1 = sem("ld_x0"), sem("ld_x1")
        ld_wq, ld_wk, ld_wv = ([sem(f"{w}{h}") for h in range(2)] for w in ("ld_wq", "ld_wk", "ld_wv"))
        ld_ctx0, ld_ctx1 = sem("ld_ctx0"), sem("ld_ctx1")
        ld_wo, ld_ffn, ld_rows = sem("ld_wo"), sem("ld_ffn"), sem("ld_rows")
        ld_cv = [sem("ld_cv0"), sem("ld_cv1")]
        consts_made = sem("consts_made")
        ctx_hi_made, ctx_lo_made = sem("ctx_hi_made"), sem("ctx_lo_made")
        ctx_rest = sem("ctx_rest")
        wk_hi_made, wk_lo_made = sem("wk_hi_made"), sem("wk_lo_made")
        wq_hi_made, wq_lo_made = sem("wq_hi_made"), sem("wq_lo_made")
        wv_hi_made, wv_lo_made = sem("wv_hi_made"), sem("wv_lo_made")
        w_rest = sem("w_rest")
        ln1_stats, ln1_aggr, ln1_eps, ln1_rstd = sem("ln1_stats"), sem("ln1_aggr"), sem("ln1_eps"), sem("ln1_rstd")
        xn_made, xT_done, xT_hi_made, xT_lo_made = sem("xn_made"), sem("xT_done"), sem("xT_hi_made"), sem("xT_lo_made")
        xbo_made = sem("xbo_made")
        q_done, q_hi_made, q_lo_made = sem("q_done"), sem("q_hi_made"), sem("q_lo_made")
        q_doubled = [sem("q_doubled0"), sem("q_doubled1")]
        k_done, k_hi_made, k_lo_made = sem("k_done"), sem("k_hi_made"), sem("k_lo_made")
        v_done, v_kept = sem("v_done"), sem("v_kept")
        scored, maxed, exped = sem("scored"), sem("maxed"), sem("exped")
        rden_made, normed, transposed = sem("rden_made"), sem("normed"), sem("transposed")
        ptr_kept = sem("ptr_kept")
        pv_done, attn_kept, wo_done = sem("pv_done"), sem("attn_kept"), sem("wo_done")
        ln2_stats, ln2_aggr, ln2_eps, ln2_rstd = (sem(s) for s in ("ln2_stats", "ln2_aggr", "ln2_eps", "ln2_rstd"))
        t_made, tb2_made = sem("t_made"), sem("tb2_made")
        ffn_done = sem("ffn_done")
        ffn_kept = sem("ffn_kept")
        ln3_stats, ln3_aggr, ln3_eps, ln3_rstd = (sem(s) for s in ("ln3_stats", "ln3_aggr", "ln3_eps", "ln3_rstd"))
        wo_kept = sem("wo_kept")
        xn_centred, t_centred, y_centred, y_normed = (sem(s) for s in ("xn_centred", "t_centred", "y_centred", "y_normed"))
        x2b_made, yg_made = sem("x2b_made"), sem("yg_made")
        out_made, stored = sem("out_made"), sem("stored")
        tail_pv, tail_attn, tail_wo, tail_x2 = sem("tail_pv"), sem("tail_attn"), sem("tail_wo"), sem("tail_x2")
        tail_tT, tail_tT_kept, tail_hid = sem("tail_tT"), sem("tail_tT_kept"), sem("tail_hid")
        tail_relu = [sem("tail_relu_act"), sem("tail_relu_dve")]
        tail_y, tail_y_kept = sem("tail_y"), sem("tail_y_kept")

        def cols(b, n):
            return slice(b * n, b * n + n) if isinstance(b, int) else bass.ds(b * n, n)

        def after(b):
            return nc.s_assert_within(b + 1, 1, B - 1,
                                      skip_runtime_bounds_check_because="used only where b < B - 1")

        def before(b):
            return (b * (B - 1)) // B

        def when(eng, holds, cond, emit):
            if holds:
                emit()
            else:
                with eng.If(cond()):
                    emit()

        block = ctx.enter_context(nc.Block())

        @block.sync
        def _(sp):
            xt = x.rearrange("(t p) d -> p t d", p=P)
            sp.dma_start(x_sb[:, 0:TT, :], xt[:, 0:TT, :]).then_inc(ld_x0, 16)
            lower, upper = slice(0, HALF), slice(HALF, INNER)
            sp.dma_start(wk_sb[:, lower], Wk[:, lower]).then_inc(ld_wk[0], 16)
            sp.dma_start(wq_sb[:, lower], Wq[:, lower]).then_inc(ld_wq[0], 16)
            sp.dma_start(wv_sb[:, lower], Wv[:, lower]).then_inc(ld_wv[0], 16)
            sp.dma_start(x_sb[:, TT:NT, :], xt[:, TT:NT, :]).then_inc(ld_x1, 16)
            sp.dma_start(wv_sb[:, upper], Wv[:, upper]).then_inc(ld_wv[1], 16)
            sp.dma_start(wk_sb[:, upper], Wk[:, upper]).then_inc(ld_wk[1], 16)
            sp.dma_start(wq_sb[:, upper], Wq[:, upper]).then_inc(ld_wq[1], 16)
            sp.dma_start(ctx_sb[:, NK:NKB], ctxT[:, NK:NKB]).then_inc(ld_ctx1, 16)

            def double_queries(u, par):
                sp.wait_ge(q_hi_made, u + 1)
                for h in range(2):
                    src, dst = slice(h * DH, h * DH + DH), slice(DH - h * DH, P - h * DH)
                    sp.dma_start(q_hh[dst, par, h, :].bitcast(F32), q_hh[src, par, h, :].bitcast(F32)).then_inc(q_doubled[par], 16)

            def move_context(half, bb):
                for dst, src in ((cv_hi[half], ctx_hi), (cv_lo[half], ctx_lo)):
                    sp.dma_start(dst[:, :].bitcast(F32), src[:, cols(bb, NK)].bitcast(F32)).then_inc(ld_cv[half], 16)

            sp.wait_ge(ctx_hi_made, 1)
            sp.wait_ge(ctx_lo_made, 1)
            move_context(1, 0)
            double_queries(1, 1)
            sp.dma_start(wo_sb[:, :, :], Wo.rearrange("(q p) d -> p q d", p=P)).then_inc(ld_wo, 16)
            for k, row in enumerate((bo, b2, gamma, beta)):
                sp.dma_start(rows[:, k, :], row.partition_broadcast(P)).then_inc(ld_rows, 16)
            sp.dma_start(w1_sb[:, :], w1).then_inc(ld_ffn, 16)
            sp.dma_start(w2_sb[:, :, :], w2.rearrange("(c p) d -> p c d", p=P)).then_inc(ld_ffn, 16)
            sp.dma_start(b1_sb[:, :], b1T).then_inc(ld_ffn, 16)

            def store(fb):
                sp.dma_start(out[cols(fb, NQ), :].rearrange("(t p) d -> p t d", p=P),
                             out_sb[:, cols(fb, TT), :]).then_inc(stored, 16)

            with sp.Fori(0, B) as b:
                for p in range(PAIRS):
                    when(sp, p < PAIRS - 2, lambda: b < B - 1,
                         lambda: double_queries(b * PAIRS + p + 2, p % 2))
                    if p == 2:
                        with sp.If(b < B - 1):
                            sp.wait_ge(ctx_rest, b * 2 + 2)
                            sp.wait_ge(v_done, b * 8 + 4)
                            move_context(0, after(b))
                    if p == 4:
                        with sp.If(b < B - 1):
                            sp.wait_ge(v_done, b * 8 + 8)
                            move_context(1, after(b))
                    if p == 1:
                        with sp.If(b > 1):
                            sp.wait_ge(out_made, before(b) * TT + 1)
                            store(before(before(b)))
            sp.wait_ge(out_made, (B - 1) * TT + 1)
            store(B - 2)
            for t in range((B - 1) * TT, NT):
                sp.wait_ge(out_made, t + 2)
                sp.dma_start(out[t * P:t * P + P, :], out_sb[:, t, :]).then_inc(stored, 16)
            sp.wait_ge(stored, 16 * (B - 1 + TT))

        @block.gpsimd
        def _(pool):
            nc.gpsimd.memset(ident[:, :], 0.0).then_inc(consts_made, 1)
            nc.gpsimd.memset(neghalf[:, :], -0.5).then_inc(consts_made, 1)
            nc.gpsimd.memset(eps[:, :], EPS).then_inc(consts_made, 1)
            pool.wait_ge(consts_made, 3)
            nc.gpsimd.affine_select(out=ident[:, :], in_=ident[:, :], compare_op=ALU.not_equal, fill=1.0,
                                    base=0, pattern=[[-1, P]], channel_multiplier=1).then_inc(consts_made, 1)

            def rstd1(g):
                tiles = slice(*LN_GROUPS[g])
                pool.wait_ge(ln1_aggr, tiles.stop)
                nc.gpsimd.tensor_tensor(ve1[:, tiles], mv1[:, tiles, 1], eps[:, tiles], ALU.add).then_inc(ln1_eps, 1)
                pool.wait_ge(ln1_eps, g + 1)
                nc.gpsimd.tensor_tensor(rs1[:, tiles], ve1[:, tiles], neghalf[:, tiles], ALU.pow).then_inc(ln1_rstd, 1)

            def split(hi, lo, full, s_made, base):
                nc.gpsimd.tensor_copy(hi, full).then_inc(s_made, 1)
                pool.wait_ge(s_made, base + 1)
                nc.gpsimd.tensor_tensor(lo, full, hi.bitcast(F32), ALU.subtract).then_inc(s_made, 1)

            rstd1(0)
            upper = slice(HALF, INNER)
            pool.wait_ge(ld_wv[1], 16)
            split(wv_hi[:, upper], wv_lo[:, upper], wv_sb[:, upper], w_rest, 0)
            pool.wait_ge(ld_wk[1], 16)
            split(wk_hi[:, upper], wk_lo[:, upper], wk_sb[:, upper], w_rest, 2)
            pool.wait_ge(ld_wq[1], 16)
            split(wq_hi[:, upper], wq_lo[:, upper], wq_sb[:, upper], w_rest, 4)

            def centre(dst, src, mv, s_made):
                shape = list(src.shape)
                nc.gpsimd.tensor_tensor(dst, src, mv[:, :, 0:1].to_broadcast(shape), ALU.subtract).then_inc(s_made, 1)

            def scale(dst, src, rs, s_made, n):
                shape = list(src.shape)
                nc.gpsimd.tensor_tensor(dst, src, rs.unsqueeze(2).to_broadcast(shape), ALU.mult).then_inc(s_made, n)

            pool.wait_ge(ld_ctx1, 16)
            for b in range(1, B):
                c = cols(b, NK)
                split(ctx_hi[:, c], ctx_lo[:, c], ctx_sb[:, c], ctx_rest, 2 * b - 2)
                if b == 1:
                    rstd1(1)
                    centre(xn_cent[:, :, :], x_sb[:, TT:NT, :], mv1[:, TT:NT, :], xn_centred)
                    pool.wait_ge(ln1_rstd, 2)
                    pool.wait_ge(xn_centred, 1)
                    scale(xn[:, TT:NT, :], xn_cent[:, :, :], rs1[:, TT:NT], xn_made, NT - TT)
            pool.wait_ge(ld_rows, 4 * 16)
            pool.wait_ge(ld_x0, 16)
            pool.wait_ge(ld_x1, 16)
            nc.gpsimd.tensor_tensor(xbo[:, :, :], x_sb[:, :, :],
                                    bo_b.unsqueeze(1).to_broadcast([P, NT, D]), ALU.add).then_inc(xbo_made, 1)

            def per_tile(row):
                return row.unsqueeze(1).to_broadcast([P, TT, D])

            with pool.Fori(0, B - 1) as b:
                pool.wait_ge(ln2_aggr, b * TT + TT)
                nc.gpsimd.tensor_tensor(ve2[:, :], mv2[:, :, 1], eps[:, 0:TT], ALU.add).then_inc(ln2_eps, 1)
                pool.wait_ge(ln2_eps, b + 1)
                nc.gpsimd.tensor_tensor(rs2[:, :], ve2[:, :], neghalf[:, 0:TT], ALU.pow).then_inc(ln2_rstd, 1)
                centre(t_cent[:, :, :], x2[:, :, :], mv2, t_centred)
                pool.wait_ge(ln2_rstd, b + 1)
                pool.wait_ge(t_centred, b + 1)
                scale(t_sb[:, :, :], t_cent[:, :, :], rs2[:, :], t_made, TT)
                nc.gpsimd.tensor_tensor(x2b[:, :, :], x2[:, :, :], per_tile(beta_b), ALU.add).then_inc(x2b_made, 1)
                pool.wait_ge(t_made, b * TT + TT)
                nc.gpsimd.tensor_tensor(tb2[:, :, :], t_sb[:, :, :], per_tile(b2_b), ALU.add).then_inc(tb2_made, 1)
                pool.wait_ge(ln3_aggr, b * TT + TT)
                nc.gpsimd.tensor_tensor(ve3[:, :], mv3[:, :, 1], eps[:, 0:TT], ALU.add).then_inc(ln3_eps, 1)
                pool.wait_ge(ln3_eps, b + 1)
                nc.gpsimd.tensor_tensor(rs3[:, :], ve3[:, :], neghalf[:, 0:TT], ALU.pow).then_inc(ln3_rstd, 1)
                centre(y_cent[:, :, :], y_sb[:, :, :], mv3, y_centred)
                pool.wait_ge(ln3_rstd, b + 1)
                pool.wait_ge(y_centred, b + 1)
                scale(y_norm[:, :, :], y_cent[:, :, :], rs3[:, :], y_normed, 1)
                pool.wait_ge(y_normed, b + 1)
                nc.gpsimd.tensor_tensor(yg[:, :, :], y_norm[:, :, :], per_tile(gamma_b), ALU.mult).then_inc(yg_made, TT)
                pool.wait_ge(yg_made, b * TT + TT)
                pool.wait_ge(x2b_made, b + 1)
                nc.gpsimd.tensor_tensor(out_sb[:, cols(b, TT), :], yg[:, :, :], x2b[:, :, :], ALU.add).then_inc(out_made, TT)

            def rstd_of_tile(ve, rs, mv, t, s_aggr, s_eps, s_rstd):
                pool.wait_ge(s_aggr, (B - 1) * TT + t + 1)
                nc.gpsimd.tensor_tensor(ve[:, t:t + 1], mv[:, t, 1:2], eps[:, 0:1], ALU.add).then_inc(s_eps, 1)
                pool.wait_ge(s_eps, B + t)
                nc.gpsimd.tensor_tensor(rs[:, t:t + 1], ve[:, t:t + 1], neghalf[:, 0:1], ALU.pow).then_inc(s_rstd, 1)

            for t in range(TT):
                rstd_of_tile(ve2, rs2, mv2, t, ln2_aggr, ln2_eps, ln2_rstd)
            for t in range(TT):
                nc.gpsimd.tensor_tensor(x2b[:, t, :], x2[:, t, :], beta_b, ALU.add).then_inc(x2b_made, 1)
                pool.wait_ge(t_made, (B - 1) * TT + t + 1)
                nc.gpsimd.tensor_tensor(tb2[:, t, :], t_sb[:, t, :], b2_b, ALU.add).then_inc(tb2_made, 1)
            for t in range(TT):
                rstd_of_tile(ve3, rs3, mv3, t, ln3_aggr, ln3_eps, ln3_rstd)

        @block.scalar
        def _(act):
            act.dma_start(ctx_sb[:, 0:NK], ctxT[:, 0:NK]).then_inc(ld_ctx0, 16)

            def keep_xT_hi(g, src):
                lo, hi = XT_GROUPS[g]
                act.wait_ge(xT_done, g + 1)
                nc.scalar.activation(xnT_hi[:, lo * P:hi * P], src[:, 0:(hi - lo) * P], ACT.Copy).then_inc(xT_hi_made, 1)

            def keep_q_hi(u, par, src=q_bank):
                act.wait_ge(q_done, u + 1)
                for h in range(2):
                    r = slice(h * DH, h * DH + DH)
                    ins = nc.scalar.activation(q_hh[r, par, h, :], src[r, 0:NQ], ACT.Copy, scale=SCALE)
                ins.then_inc(q_hi_made, 1)

            def keep_k_hi(u, par, heads=range(2), src=k_bank):
                act.wait_ge(k_done, u + 1)
                for h in heads:
                    r = slice(h * DH, h * DH + DH)
                    nc.scalar.activation(k_hl[r, par, h, :], src[r, :], ACT.Copy).then_inc(k_hi_made, 1)

            def keep_values(n, half, kt, src=v_bank):
                act.wait_ge(v_done, n + 1)
                nc.scalar.activation(values[:, kt, half * HALF:half * HALF + HALF], src[:, :],
                                     ACT.Copy).then_inc(v_kept, 1)

            def exp_tile(n, par, i):
                act.wait_ge(maxed, n + 1)
                nc.scalar.activation(probs[:, i, :], score_bank[i % 2][:, :], ACT.Exp, bias=negmax[:, par, i:i + 1],
                                     accum_out=den[:, par, i:i + 1]).then_inc(exped, 1)

            def keep_transposed(n, par, i, src=ptr_bank):
                h, qt = i // QT, i % QT
                act.wait_ge(transposed, n + 1)
                nc.scalar.activation(probsT[:, par, h, :, qt * P:qt * P + P],
                                     src[:, :].rearrange("k (t q) -> k t q", t=KT),
                                     ACT.Copy).then_inc(ptr_kept, 1)

            def keep_tT(fb):
                act.wait_ge(ffn_done, fb * 4 + 1)
                nc.scalar.activation(tT[:, :], v_bank[:, 0:NQ], ACT.Copy).then_inc(ffn_kept, 1)

            def keep_hidden(fb, k):
                act.wait_ge(ld_ffn, 3 * 16)
                act.wait_ge(ffn_done, fb * 4 + 2 + k)
                for j in range(2):
                    c = 2 * k + j
                    ins = nc.scalar.activation(hid[:, c, :], v_bank[:, j * NQ:j * NQ + NQ], ACT.Relu,
                                               bias=b1_sb[:, c:c + 1])
                ins.then_inc(ffn_kept, 1)

            def high_half(hi, full, s_loaded, s_made):
                act.wait_ge(s_loaded, 16)
                nc.scalar.activation(hi, full, ACT.Copy).then_inc(s_made, 1)

            high_half(ctx_hi[:, 0:NK], ctx_sb[:, 0:NK], ld_ctx0, ctx_hi_made)
            high_half(wk_hi[:, 0:HALF], wk_sb[:, 0:HALF], ld_wk[0], wk_hi_made)
            high_half(wq_hi[:, 0:HALF], wq_sb[:, 0:HALF], ld_wq[0], wq_hi_made)
            high_half(wv_hi[:, 0:HALF], wv_sb[:, 0:HALF], ld_wv[0], wv_hi_made)
            keep_xT_hi(0, ptr_bank)
            keep_k_hi(0, 0)
            keep_q_hi(0, 0)
            act.wait_ge(q_hi_made, 1)
            for h in range(2):
                r, across = slice(h * DH, h * DH + DH), slice(DH - h * DH, P - h * DH)
                ins = nc.scalar.activation(q_hh[across, 0, h, :], q_hh[r, 0, h, :].bitcast(F32), ACT.Copy)
            ins.then_inc(q_doubled[0], 32)
            keep_k_hi(1, 1, range(2), pv_bank)
            keep_q_hi(1, 1, wo_bank)
            exp_tile(0, 0, 0)
            keep_values(0, 0, 0)
            exp_tile(1, 0, 1)
            keep_values(1, 0, 1, ptr_bank)
            exp_tile(2, 0, 2)
            keep_values(2, 0, 2, pv_bank)
            exp_tile(3, 0, 3)
            keep_values(3, 0, 3)

            with act.Fori(0, B) as b:
                def slot(p):
                    par, nxt = p % 2, (p + 1) % 2
                    n = b * (4 * PAIRS) + 4 * p
                    for i in range(4):
                        keep_transposed(n + i, par, i)
                        if i == 2:
                            when(act, p < PAIRS - 2, lambda: b < B - 1,
                                 lambda: keep_k_hi(b * PAIRS + p + 2, par, (1,)))
                        when(act, p < PAIRS - 1, lambda: b < B - 1, lambda: exp_tile(n + 4 + i, nxt, i))
                        if i == 0:
                            when(act, p < PAIRS - 2, lambda: b < B - 1,
                                 lambda: keep_q_hi(b * PAIRS + p + 2, par))
                        if i == 1:
                            when(act, p < PAIRS - 2, lambda: b < B - 1,
                                 lambda: keep_k_hi(b * PAIRS + p + 2, par, (0,)))
                            if p in (4, 5):
                                when(act, False, lambda: b < 1, lambda: keep_xT_hi(p - 3, v_bank))
                            if p == 3:
                                when(act, False, lambda: b > 0, lambda: keep_tT(before(b)))
                            if p in (4, 5):
                                when(act, False, lambda: b > 0, lambda: keep_hidden(before(b), p - 4))
                    when(act, p < 4, lambda: b < B - 1,
                         lambda: keep_values(b * 8 + 4 + p, 1 if p < 4 else 0, p % 4))

                for p in range(PAIRS):
                    when(act, p < PAIRS - 1, lambda: b < B - 1, lambda: slot(p))

            for i in range(4):
                keep_transposed(UNITS * 4 - 4 + i, 1, i, last_ptr[i])
            for t in range(TT):
                act.wait_ge(tail_tT, t + 1)
                nc.scalar.activation(tT[:, t * P:t * P + P], tail_tT_bank[t][:, 0:P], ACT.Copy).then_inc(tail_tT_kept, 1)
                act.wait_ge(tail_hid, 2 * t + 1)
                for c in (0, 1):
                    ins = nc.scalar.activation(hid[:, c, t * P:t * P + P], tail_hid_bank[t][0][:, c * P:c * P + P],
                                               ACT.Relu, bias=b1_sb[:, c:c + 1])
                ins.then_inc(tail_relu[0], 1)

        @block.vector
        def _(dve):
            def stats(st, mv, src, tiles, s_stats, s_aggr, base, carrier=None):
                for k, t in enumerate(tiles):
                    nc.vector.bn_stats(st[:, t, :], src[:, t, :]).then_inc(s_stats, 1)
                for k, t in enumerate(tiles):
                    if isinstance(base, int):
                        dve.wait_ge(s_stats, base + k + 1)
                    elif k == 0:
                        dve.wait_ge(s_stats, base + len(tiles))
                        nc.vector.memset(carrier[:, :], 0.0)
                    nc.vector.bn_aggr(mv[:, t, :], st[:, t, :]).then_inc(s_aggr, 1)

            def apply_norm(dst, src, mv, rs, t, s_made):
                nc.vector.tensor_scalar(dst[:, t, :], src[:, t, :], mv[:, t, 0:1], rs[:, t:t + 1],
                                        ALU.subtract, ALU.mult).then_inc(s_made, 1)

            def low_half(lo, full, hi, s_made):
                nc.vector.tensor_tensor(lo, full, hi.bitcast(F32), ALU.subtract).then_inc(s_made, 1)

            def keep_xT_lo(g, src):
                lo, hi = XT_GROUPS[g]
                dve.wait_ge(xT_hi_made, g + 1)
                low_half(xnT_lo[:, lo * P:hi * P], src[:, 0:(hi - lo) * P], xnT_hi[:, lo * P:hi * P], xT_lo_made)

            def keep_q_lo(u, par, src=q_bank):
                dve.wait_ge(q_hi_made, u + 1)
                for h in range(2):
                    r = slice(h * DH, h * DH + DH)
                    ins = nc.vector.scalar_tensor_tensor(out=q_lo[r, par, :], in0=src[r, 0:NQ], scalar=SCALE,
                                                         in1=q_hh[r, par, h, :].bitcast(F32),
                                                         op0=ALU.mult, op1=ALU.subtract)
                ins.then_inc(q_lo_made, 1)

            def keep_k_lo(u, par, src=k_bank):
                for h in range(2):
                    dve.wait_ge(k_hi_made, u * 2 + h + 1)
                    r, across = slice(h * DH, h * DH + DH), slice(DH - h * DH, P - h * DH)
                    ins = nc.vector.tensor_tensor(k_hl[across, par, h, :], src[r, :],
                                                  k_hl[r, par, h, :].bitcast(F32), ALU.subtract)
                ins.then_inc(k_lo_made, 1)

            def row_max(n, par, i):
                dve.wait_ge(scored, n + 1)
                nc.vector.tensor_reduce(negmax[:, par, i:i + 1], score_bank[i % 2][:, :], AX_X, ALU.max,
                                        negate=True).then_inc(maxed, 1)

            def row_rden(n, par, i):
                dve.wait_ge(exped, n + 1)
                nc.vector.reciprocal(rden[:, par, i:i + 1], den[:, par, i:i + 1]).then_inc(rden_made, 1)

            def row_norm(n, par, i):
                dve.wait_ge(rden_made, n + 1)
                nc.vector.tensor_scalar(probs[:, i, :], probs[:, i, :], rden[:, par, i:i + 1], None,
                                        ALU.mult).then_inc(normed, 1)

            def keep_attn(u, par):
                dve.wait_ge(pv_done, u + 1)
                nc.vector.tensor_copy(attnT[:, par, :], pv_bank[:, 0:NQ]).then_inc(attn_kept, 1)

            def residual(fb):
                dve.wait_ge(wo_done, fb * PAIRS + PAIRS)
                dve.wait_ge(xbo_made, 1)
                dve.wait_ge(out_made, fb * TT + 1)
                xr = xbo[:, bass.ds(fb * TT, TT), :]
                nc.vector.tensor_tensor(x2[:, :, :], wo_bank[:, 0:NQ].rearrange("p (t d) -> p t d", t=TT), xr,
                                        ALU.add).then_inc(wo_kept, 1)

            def residual_stats(fb):
                dve.wait_ge(wo_kept, fb + 2)
                stats(st2, mv2, x2, range(TT), ln2_stats, ln2_aggr, fb * TT, carrier2)

            def finish_y(fb, done):
                dve.wait_ge(ffn_done, done)
                dve.wait_ge(tb2_made, fb + 1)
                nc.vector.tensor_tensor(y_sb[:, :, :], v_bank[:, 0:NQ].rearrange("p (t d) -> p t d", t=TT),
                                        tb2[:, :, :], ALU.add).then_inc(ffn_kept, 1)

            def y_stats(fb, kept):
                dve.wait_ge(ffn_kept, kept)
                stats(st3, mv3, y_sb, range(TT), ln3_stats, ln3_aggr, fb * TT, carrier3)

            def scale_centred(t):
                nc.vector.scalar_tensor_tensor(out=yg[:, t, :], in0=y_sb[:, t, :], scalar=mv3[:, t, 0:1],
                                               in1=gamma_b, op0=ALU.subtract, op1=ALU.mult).then_inc(yg_made, 1)

            def add_x2(fb, t):
                dve.wait_ge(yg_made, fb * TT + t + 1)
                nc.vector.scalar_tensor_tensor(out=out_sb[:, fb * TT + t, :], in0=yg[:, t, :], scalar=rs3[:, t:t + 1],
                                               in1=x2b[:, t, :], op0=ALU.mult, op1=ALU.add).then_inc(out_made, 1)

            nc.vector.memset(credits[:, 0:1], 0.0).then_inc(ffn_kept, 4)
            nc.vector.memset(credits[:, 1:2], 0.0).then_inc(wo_kept, 1)
            nc.vector.memset(credits[:, 2:3], 0.0).then_inc(out_made, 1)
            nc.vector.memset(credits[:, 3:4], 0.0).then_inc(ptr_kept, 1)

            def stats1(lo, hi):
                stats(st1, mv1, x_sb, range(lo, hi), ln1_stats, ln1_aggr, lo)

            dve.wait_ge(ld_x0, 16)
            stats1(0, TT)
            dve.wait_ge(ctx_hi_made, 1)
            low_half(ctx_lo[:, 0:NK], ctx_sb[:, 0:NK], ctx_hi[:, 0:NK], ctx_lo_made)
            dve.wait_ge(wk_hi_made, 1)
            low_half(wk_lo[:, 0:HALF], wk_sb[:, 0:HALF], wk_hi[:, 0:HALF], wk_lo_made)
            dve.wait_ge(ln1_rstd, 1)
            for t in range(TT):
                apply_norm(xn, x_sb, mv1, rs1, t, xn_made)
            dve.wait_ge(wq_hi_made, 1)
            low_half(wq_lo[:, 0:HALF], wq_sb[:, 0:HALF], wq_hi[:, 0:HALF], wq_lo_made)
            keep_xT_lo(0, ptr_bank)
            dve.wait_ge(ld_x1, 16)
            stats1(TT, 4)
            keep_k_lo(0, 0)
            keep_q_lo(0, 0)
            dve.wait_ge(wv_hi_made, 1)
            low_half(wv_lo[:, 0:HALF], wv_sb[:, 0:HALF], wv_hi[:, 0:HALF], wv_lo_made)
            row_max(0, 0, 0)
            row_max(1, 0, 1)
            keep_k_lo(1, 1, pv_bank)
            row_rden(0, 0, 0)
            row_norm(0, 0, 0)
            row_max(2, 0, 2)
            keep_q_lo(1, 1, wo_bank)
            row_rden(1, 0, 1)
            row_norm(1, 0, 1)
            row_rden(2, 0, 2)
            row_max(3, 0, 3)
            row_norm(2, 0, 2)

            with dve.Fori(0, B) as b:
                def slot(p):
                    par, nxt = p % 2, (p + 1) % 2
                    n = b * (4 * PAIRS) + 4 * p
                    for i in range(4):
                        if i == 0:
                            row_rden(n + 3, par, 3)
                        if i == 3:
                            when(dve, p > 0, lambda: b > 0, lambda: keep_attn(b * PAIRS + p - 1, nxt))

                        def sums_and_max():
                            if i:
                                row_rden(n + 4 + i - 1, nxt, i - 1)
                            row_max(n + 4 + i, nxt, i)
                        when(dve, p < PAIRS - 1, lambda: b < B - 1, sums_and_max)
                        if i == 1:
                            when(dve, p < PAIRS - 2, lambda: b < B - 1,
                                 lambda: keep_q_lo(b * PAIRS + p + 2, par))
                        if i == 2:
                            if p == 6:
                                when(dve, False, lambda: b > 0, lambda: finish_y(before(b), before(b) * 4 + 4))
                            if p in (4, 5):
                                when(dve, False, lambda: b < 1, lambda: keep_xT_lo(p - 3, v_bank))
                            when(dve, p < PAIRS - 2, lambda: b < B - 1,
                                 lambda: keep_k_lo(b * PAIRS + p + 2, par))
                        if i == 0:
                            row_norm(n + 3, par, 3)
                        else:
                            when(dve, p < PAIRS - 1, lambda: b < B - 1,
                                 lambda: row_norm(n + 4 + i - 1, nxt, i - 1))
                        if i == 3 and p in (1, 2):
                            when(dve, False, lambda: b < 1, lambda: stats1(2 * p + 2, 2 * p + 4))
                        if i == 1 and p == 1:
                            when(dve, False, lambda: b > 0, lambda: residual(before(b)))
                        if i == 3 and p == 1:
                            when(dve, False, lambda: b > 0, lambda: residual_stats(before(b)))
                        if i == 3 and p == 6:
                            when(dve, False, lambda: b > 0, lambda: y_stats(before(b), before(b) * 4 + 8))

                for p in range(PAIRS):
                    when(dve, p < PAIRS - 1, lambda: b < B - 1, lambda: slot(p))

            row_rden(UNITS * 4 - 1, 1, 3)
            row_norm(UNITS * 4 - 1, 1, 3)
            keep_attn(UNITS - 2, 0)

            def tail_keep_attn(t):
                dve.wait_ge(tail_pv, t + 1)
                nc.vector.tensor_copy(attnT[:, 1, t * P:t * P + P], tail_pv_bank[t][:, 0:P]).then_inc(tail_attn, 1)

            def stats_of_tile(st, mv, src, t, s_stats, s_aggr):
                nc.vector.bn_stats(st[:, t, :], src[:, t, :]).then_inc(s_stats, 1)
                dve.wait_ge(s_stats, (B - 1) * TT + t + 1)
                nc.vector.bn_aggr(mv[:, t, :], st[:, t, :]).then_inc(s_aggr, 1)

            def tail_residual(t):
                dve.wait_ge(tail_wo, t + 1)
                nc.vector.tensor_tensor(x2[:, t, :], wo_bank[:, t * D:t * D + D], xbo[:, (B - 1) * TT + t, :],
                                        ALU.add).then_inc(tail_x2, 1)
                dve.wait_ge(tail_x2, t + 1)
                stats_of_tile(st2, mv2, x2, t, ln2_stats, ln2_aggr)

            def tail_norm2(t):
                dve.wait_ge(ln2_rstd, B + t)
                apply_norm(t_sb, x2, mv2, rs2, t, t_made)

            dve.wait_ge(out_made, (B - 1) * TT + 1)
            tail_keep_attn(0)
            tail_residual(0)
            tail_keep_attn(1)
            tail_norm2(0)
            tail_residual(1)
            tail_norm2(1)
            for t in range(TT):
                dve.wait_ge(tail_hid, 2 * t + 2)
                for c in (2, 3):
                    ins = nc.vector.tensor_scalar(hid[:, c, t * P:t * P + P],
                                                  tail_hid_bank[t][1][:, (c - 2) * P:(c - 2) * P + P],
                                                  b1_sb[:, c:c + 1], 0.0, ALU.add, ALU.max)
                ins.then_inc(tail_relu[1], 1)
            for t in range(TT):
                dve.wait_ge(tail_y, t + 1)
                dve.wait_ge(tb2_made, B + t)
                nc.vector.tensor_tensor(y_sb[:, t, :], tail_y_bank[t][:, 0:D], tb2[:, t, :],
                                        ALU.add).then_inc(tail_y_kept, 1)
                dve.wait_ge(tail_y_kept, t + 1)
                stats_of_tile(st3, mv3, y_sb, t, ln3_stats, ln3_aggr)
            for t in range(TT):
                dve.wait_ge(ln3_aggr, (B - 1) * TT + t + 1)
                scale_centred(t)
            for t in range(TT):
                dve.wait_ge(ln3_rstd, B + t)
                dve.wait_ge(x2b_made, B + t)
                add_x2(B - 1, t)

        @block.tensor
        def _(pe):
            def three(dst, w, m):
                (w_hi, w_lo), (m_hi, m_lo) = w, m
                nc.tensor.matmul(dst, w_hi, m_hi, start=True, stop=False)
                nc.tensor.matmul(dst, w_hi, m_lo, start=False, stop=False)
                return nc.tensor.matmul(dst, w_lo, m_hi, start=False, stop=True)

            def transpose_x(g, dst):
                lo, hi = XT_GROUPS[g]
                pe.wait_ge(xn_made, hi)
                for t in range(lo, hi):
                    ins = nc.tensor.transpose(dst[:, (t - lo) * P:(t - lo) * P + P], xn[:, t, :], ident[:, :])
                ins.then_inc(xT_done, 1)

            def project_q(p, bb, dst=q_bank):
                c = slice(p * P, p * P + P)
                three(dst[:, 0:NQ], (wq_hi[:, c], wq_lo[:, c]),
                      (xnT_hi[:, cols(bb, NQ)], xnT_lo[:, cols(bb, NQ)])).then_inc(q_done, 1)

            def project_k(p, bb, dst=k_bank):
                c = slice(p * P, p * P + P)
                three(dst[:, :], (wk_hi[:, c], wk_lo[:, c]),
                      (ctx_hi[:, cols(bb, NK)], ctx_lo[:, cols(bb, NK)])).then_inc(k_done, 1)

            def value_piece(chi, clo, half, kt, dst=v_bank):
                k, c = slice(kt * P, kt * P + P), slice(half * HALF, half * HALF + HALF)
                three(dst[:, :], (chi[:, k], clo[:, k]), (wv_hi[:, c], wv_lo[:, c])).then_inc(v_done, 1)

            def score(par, i):
                h, qt = i // QT, i % QT
                q, r = slice(qt * P, qt * P + P), slice(h * DH, h * DH + DH)
                nc.tensor.matmul(score_bank[i % 2][:, :], q_hh[:, par, h, q], k_hl[:, par, h, :], start=True, stop=False)
                nc.tensor.matmul(score_bank[i % 2][:, :], q_lo[r, par, q], k_hl[r, par, h, :],
                                 start=False, stop=True).then_inc(scored, 1)

            def transpose_probs(i, dst=ptr_bank):
                for kt in range(KT):
                    ins = nc.tensor.transpose(dst[:, kt * P:kt * P + P], probs[:, i, kt * P:kt * P + P],
                                              ident[:, :])
                ins.then_inc(transposed, 1)

            def times_values(p, par, key_tiles):
                for kt in key_tiles:
                    for h in range(2):
                        c = (2 * p + h) * DH
                        ins = nc.tensor.matmul(pv_bank[h * DH:h * DH + DH, 0:NQ], values[:, kt, c:c + DH],
                                               probsT[:, par, h, kt, :], start=(kt == 0), stop=(kt == KT - 1))
                if kt == KT - 1:
                    ins.then_inc(pv_done, 1)

            def out_project(p, par, tiles=range(TT), s_done=wo_done):
                for t in tiles:
                    ins = nc.tensor.matmul(wo_bank[:, t * D:t * D + D], attnT[:, par, t * P:t * P + P],
                                           wo_sb[:, p, :], start=(p == 0 and t == 0), stop=(p == PAIRS - 1),
                                           skip_group_check=True)
                ins.then_inc(s_done, 1)

            def ffn_piece(k, fb):
                if k == 0:
                    pe.wait_ge(t_made, fb * TT + TT)
                    for t in range(TT):
                        ins = nc.tensor.transpose(v_bank[:, t * P:t * P + P], t_sb[:, t, :], ident[:, :])
                elif k < 3:
                    pe.wait_ge(ffn_kept, fb * 4 + 4 + k)
                    for j in range(2):
                        c = 2 * (k - 1) + j
                        ins = nc.tensor.matmul(v_bank[:, j * NQ:j * NQ + NQ], w1_sb[:, c * P:c * P + P], tT[:, :],
                                               start=True, stop=True)
                else:
                    pe.wait_ge(ffn_kept, fb * 4 + 4 + 3)
                    for t in range(TT):
                        for c in range(FC):
                            ins = nc.tensor.matmul(v_bank[:, t * D:t * D + D], hid[:, c, t * P:t * P + P],
                                                   w2_sb[:, c, :], start=(c == 0), stop=(c == FC - 1))
                ins.then_inc(ffn_done, 1)

            pe.wait_ge(ctx_lo_made, 1)
            pe.wait_ge(wk_lo_made, 1)
            project_k(0, 0)
            pe.wait_ge(consts_made, 4)
            transpose_x(0, ptr_bank)
            project_k(1, 0, pv_bank)
            pe.wait_ge(wq_lo_made, 1)
            pe.wait_ge(xT_lo_made, 1)
            project_q(0, 0)
            project_q(1, 0, wo_bank)
            pe.wait_ge(q_lo_made, 1)
            pe.wait_ge(k_lo_made, 1)
            pe.wait_ge(q_doubled[0], 32)
            score(0, 0)
            score(0, 1)
            pe.wait_ge(wv_lo_made, 1)
            value_piece(ctx_hi, ctx_lo, 0, 0)
            value_piece(ctx_hi, ctx_lo, 0, 1, ptr_bank)
            pe.wait_ge(exped, 1)
            score(0, 2)
            pe.wait_ge(k_lo_made, 2)
            value_piece(ctx_hi, ctx_lo, 0, 2, pv_bank)
            pe.wait_ge(exped, 2)
            score(0, 3)
            pe.wait_ge(v_kept, 1)
            value_piece(ctx_hi, ctx_lo, 0, 3)
            pe.wait_ge(q_lo_made, 2)
            pe.wait_ge(v_kept, 2)

            with pe.Fori(0, B) as b:
                def slot(p):
                    par, nxt = p % 2, (p + 1) % 2
                    u = b * PAIRS + p
                    n = b * (4 * PAIRS) + 4 * p
                    for i in range(4):
                        def next_score():
                            pe.wait_ge(exped, n + i + 3)
                            if i == 0:
                                pe.wait_ge(q_lo_made, u + 2)
                                pe.wait_ge(k_lo_made, u + 2)
                                pe.wait_ge(q_doubled[nxt], b * (32 * PAIRS // 2) + 32 * ((p + 1) // 2 + 1))
                            score(nxt, i)
                        when(pe, p < PAIRS - 1, lambda: b < B - 1, next_score)

                        pe.wait_ge(normed, n + i + 1)
                        pe.wait_ge(ptr_kept, n + i + 1)
                        transpose_probs(i)

                        if i == 0:
                            def next_queries():
                                if p == 2:
                                    pe.wait_ge(w_rest, 6)
                                project_q((p + 2) % PAIRS, b if p < PAIRS - 2 else after(b))
                            when(pe, p < PAIRS - 2, lambda: b < B - 1, next_queries)

                            def out_project_before():
                                pe.wait_ge(attn_kept, before(b) * PAIRS + PAIRS - 1 if p == 0 else u - 1)
                                if p == 2:
                                    pe.wait_ge(wo_kept, b + 1)
                                out_project((p - 2) % PAIRS, par)
                            when(pe, p > 1, lambda: b > 0, out_project_before)

                            def prev_values():
                                if p == 1:
                                    pe.wait_ge(ld_wo, 16)
                                    pe.wait_ge(ld_ffn, 3 * 16)
                                if p in (1, 5):
                                    pe.wait_ge(v_kept, b * 8 + 4 + p - 1)
                                times_values((p - 1) % PAIRS, nxt, range(0, KT // 2))
                            when(pe, p > 0, lambda: b > 0, prev_values)
                        if i == 1:
                            def next_keys():
                                if p == 6:
                                    pe.wait_ge(ctx_rest, b * 2 + 2)
                                project_k((p + 2) % PAIRS, b if p < PAIRS - 2 else after(b))
                            when(pe, p < PAIRS - 2, lambda: b < B - 1, next_keys)

                            def other_queries():
                                pe.wait_ge(v_kept, b * 8 + 4 + p)
                                transpose_x(p - 3, v_bank)
                            if p in (4, 5):
                                when(pe, False, lambda: b < 1, other_queries)

                            def next_ffn_piece():
                                when(pe, p < 5, lambda: b < B - 1, lambda: pe.wait_ge(v_kept, b * 8 + 4 + p))
                                ffn_piece(p - 3, before(b))
                            if 3 <= p <= 6:
                                when(pe, False, lambda: b > 0, next_ffn_piece)
                        if i == 2:
                            when(pe, p > 0, lambda: b > 0,
                                 lambda: times_values((p - 1) % PAIRS, nxt, range(KT // 2, KT)))
                        if i == 3:
                            def next_value_piece():
                                pe.wait_ge(v_kept, b * 8 + 4 + p)
                                if p in (4, 5):
                                    pe.wait_ge(xT_lo_made, p - 2)
                                if 3 <= p <= 6:
                                    pe.wait_ge(ffn_kept, b * 4 + p - 2)
                                if p == 0:
                                    pe.wait_ge(w_rest, 2)
                                half = 1 if p < 4 else 0
                                pe.wait_ge(ld_cv[half], (b + 1) * 32)
                                value_piece(cv_hi[half], cv_lo[half], half, p % 4)
                            when(pe, p < 4, lambda: b < B - 1, next_value_piece)

                for p in range(PAIRS):
                    when(pe, p < PAIRS - 1, lambda: b < B - 1, lambda: slot(p))

            for i in range(4):
                if i == 2:
                    pe.wait_ge(ptr_kept, UNITS * 4 - 3)
                if i == 3:
                    pe.wait_ge(attn_kept, UNITS - 2)
                    out_project(PAIRS - 3, 1)
                    times_values(PAIRS - 2, 0, range(KT))
                pe.wait_ge(normed, UNITS * 4 - 3 + i)
                transpose_probs(i, last_ptr[i])

            def tail_values(t):
                for kt in range(KT):
                    for h in range(2):
                        c = (2 * (PAIRS - 1) + h) * DH
                        ins = nc.tensor.matmul(tail_pv_bank[t][h * DH:h * DH + DH, 0:P], values[:, kt, c:c + DH],
                                               probsT[:, 1, h, kt, t * P:t * P + P], start=(kt == 0), stop=(kt == KT - 1))
                ins.then_inc(tail_pv, 1)

            def tail_out_project(t):
                pe.wait_ge(tail_attn, t + 1)
                out_project(PAIRS - 1, 1, (t,), tail_wo)

            pe.wait_ge(ptr_kept, UNITS * 4)
            tail_values(0)
            pe.wait_ge(attn_kept, UNITS - 1)
            out_project(PAIRS - 2, 0)
            tail_out_project(0)
            pe.wait_ge(ptr_kept, UNITS * 4 + 1)
            tail_values(1)
            pe.wait_ge(tail_x2, 1)
            tail_out_project(1)
            for t in range(TT):
                pe.wait_ge(t_made, (B - 1) * TT + t + 1)
                nc.tensor.transpose(tail_tT_bank[t][:, 0:P], t_sb[:, t, :], ident[:, :]).then_inc(tail_tT, 1)
                pe.wait_ge(tail_tT_kept, t + 1)
                for c in range(FC):
                    ins = nc.tensor.matmul(tail_hid_bank[t][c // 2][:, c % 2 * P:c % 2 * P + P],
                                           w1_sb[:, c * P:c * P + P], tT[:, t * P:t * P + P], start=True, stop=True)
                    if c % 2 == 1:
                        ins.then_inc(tail_hid, 1)
            for t in range(TT):
                for c in range(FC):
                    if c % 2 == 0:
                        pe.wait_ge(tail_relu[c // 2], t + 1)
                    ins = nc.tensor.matmul(tail_y_bank[t][:, 0:D], hid[:, c, t * P:t * P + P], w2_sb[:, c, :],
                                           start=(c == 0), stop=(c == FC - 1))
                ins.then_inc(tail_y, 1)


def kernel(x, ctx_768, L0_xattn_Wq, L0_xattn_Wk, L0_xattn_Wv, L0_xattn_Wo, L0_xattn_bo,
           L0_ffn_router_w, L0_ffn_router_b, L0_ffn_w1, L0_ffn_b1, L0_ffn_w2, L0_ffn_b2,
           L0_ffn_gamma, L0_ffn_beta):
    import numpy as np
    import concourse.bacc as bacc
    from concourse.bass_utils import run_bass_kernel_spmd

    B, NQ, D = x.shape
    C = ctx_768.shape[2]
    P = 128
    arrays = {
        "x": np.asarray(x).reshape(B * NQ, D),
        "ctxT": np.asarray(ctx_768).transpose(2, 0, 1).reshape(C, -1),
        "Wq": np.asarray(L0_xattn_Wq),
        "Wk": np.asarray(L0_xattn_Wk),
        "Wv": np.asarray(L0_xattn_Wv),
        "Wo": np.asarray(L0_xattn_Wo),
        "bo": np.asarray(L0_xattn_bo),
        "w1": np.asarray(L0_ffn_w1)[0],
        "b1T": np.asarray(L0_ffn_b1)[0].reshape(-1, P).T,
        "w2": np.asarray(L0_ffn_w2)[0],
        "b2": np.asarray(L0_ffn_b2)[0],
        "gamma": np.asarray(L0_ffn_gamma),
        "beta": np.asarray(L0_ffn_beta),
    }
    arrays = {f"in_{k}": np.ascontiguousarray(v) for k, v in arrays.items()}
    nc = bacc.Bacc("TRN2", target_bir_lowering=False, num_devices=1)
    args = [nc.dram_tensor(k, v.shape, mybir.dt.from_np(v.dtype), kind="ExternalInput").ap()
            for k, v in arrays.items()]
    args.append(nc.dram_tensor("out", (B * NQ, D), F32, kind="ExternalOutput").ap())
    xattn_ffn_kernel(nc, *args)
    r = run_bass_kernel_spmd(nc, [arrays], core_ids=[0])
    return r.results[0]["out"].reshape(B, NQ, D)
```
